# Optimizing a Trainium2 kernel written in Bass

```python
import numpy as np
import jax
import jax.numpy as jnp

def _softmax(x, axis=-1):
    return jax.nn.softmax(x, axis=axis)

def _gelu(x):
    return jax.nn.gelu(x, approximate=True)

def _silu(x):
    return jax.nn.silu(x)

def _sigmoid(x):
    return jax.nn.sigmoid(x)

def _layernorm(x, axis=-1, eps=1e-05):
    m = jnp.mean(x, axis=axis, keepdims=True)
    v = jnp.var(x, axis=axis, keepdims=True)
    return (x - m) / jnp.sqrt(v + eps)

def _scatter_add(tgt, idx, src, axis=0):
    return tgt.at[idx].add(src)

def _segment_sum(src, seg, n):
    return jax.ops.segment_sum(src, seg, n)
kernel_name = 'mk_macaron_d1_jaxref_r8_2dfe1f'

def setup_inputs(seed: int=0):
    np.random.seed(seed)
    _w = jnp.asarray

    def _L0_attn_setup():
        import jax, jax.numpy as jnp
        import numpy as np
        HEADS = 16
        DIM_HEAD = 64
        SEG = 64
        THETA = 10000.0
        NEG_INF = -1e+30

        def _rotate_half(t):
            t2 = t.reshape(*t.shape[:-1], t.shape[-1] // 2, 2)
            return jnp.stack((-t2[..., 1], t2[..., 0]), axis=-1).reshape(t.shape)
        key = jax.random.key(seed)
        ks = jax.random.split(key, 4)
        b, n, d = (2, 512, 128)
        dim_inner = HEADS * DIM_HEAD
        seq = jax.random.normal(ks[0], (b, n, d), dtype=jnp.float32)
        g_norm = jnp.ones((d,), dtype=jnp.float32)
        W_qkv = jax.random.normal(ks[1], (d, 3 * dim_inner), dtype=jnp.float32) * d ** (-0.5)
        W_out = jax.random.normal(ks[2], (dim_inner, d), dtype=jnp.float32) * dim_inner ** (-0.5)
        pm = jax.random.normal(ks[3], (2, HEADS, 16, DIM_HEAD), dtype=jnp.float32) * 0.02
        return {'seq': seq, 'g_norm': g_norm, 'W_qkv': W_qkv, 'W_out': W_out, 'pm': pm}
    _L0_attn_in = _L0_attn_setup()

    def _L0_ffn_setup():
        import jax, jax.numpy as jnp
        import numpy as np
        D_MODEL = 128
        N_EXPERTS = 8
        TOP_K = 2
        HIDDEN = 4 * D_MODEL
        key = jax.random.key(seed)
        ks = jax.random.split(key, 6)
        B, S = (2, 256)
        x = jax.random.normal(ks[0], (B, S, D_MODEL), dtype=jnp.float32)
        shared_w1 = jax.random.normal(ks[1], (HIDDEN, D_MODEL), dtype=jnp.float32) * 0.02
        shared_w2 = jax.random.normal(ks[2], (D_MODEL, HIDDEN), dtype=jnp.float32) * 0.02
        experts_w1 = jax.random.normal(ks[3], (N_EXPERTS, HIDDEN, D_MODEL), dtype=jnp.float32) * 0.02
        experts_w2 = jax.random.normal(ks[4], (N_EXPERTS, D_MODEL, HIDDEN), dtype=jnp.float32) * 0.02
        gate_w = jax.random.normal(ks[5], (N_EXPERTS, D_MODEL), dtype=jnp.float32) * 0.02
        return {'x': x, 'shared_w1': shared_w1, 'shared_w2': shared_w2, 'experts_w1': experts_w1, 'experts_w2': experts_w2, 'gate_w': gate_w}
    _L0_ffn_in = _L0_ffn_setup()
    _d = {'L0_attn_seq': _L0_attn_in['seq'], 'L0_attn_g_norm': _L0_attn_in['g_norm'], 'L0_attn_W_qkv': _L0_attn_in['W_qkv'], 'L0_attn_W_out': _L0_attn_in['W_out'], 'L0_attn_pm': _L0_attn_in['pm'], 'L0_ffn_shared_w1': _L0_ffn_in['shared_w1'], 'L0_ffn_shared_w2': _L0_ffn_in['shared_w2'], 'L0_ffn_experts_w1': _L0_ffn_in['experts_w1'], 'L0_ffn_experts_w2': _L0_ffn_in['experts_w2'], 'L0_ffn_gate_w': _L0_ffn_in['gate_w']}
    _x0 = _d['L0_attn_seq']
    _d['L0_attn_seq'] = jax.random.normal(jax.random.fold_in(jax.random.key(seed), 1), (8, 256, 128), dtype=_x0.dtype)
    del _x0
    return _d

def reference(L0_attn_seq, L0_attn_g_norm, L0_attn_W_qkv, L0_attn_W_out, L0_attn_pm, L0_ffn_shared_w1, L0_ffn_shared_w2, L0_ffn_experts_w1, L0_ffn_experts_w2, L0_ffn_gate_w):

    def _L0_attn_ref(seq, g_norm, W_qkv, W_out, pm):
        import jax, jax.numpy as jnp
        import numpy as np
        HEADS = 16
        DIM_HEAD = 64
        SEG = 64
        THETA = 10000.0
        NEG_INF = -1e+30

        def _rotate_half(t):
            t2 = t.reshape(*t.shape[:-1], t.shape[-1] // 2, 2)
            return jnp.stack((-t2[..., 1], t2[..., 0]), axis=-1).reshape(t.shape)
        b, n_tot, dim = seq.shape
        p = pm.shape[2]
        dh = DIM_HEAD
        eps = jnp.asarray(jnp.finfo(seq.dtype).eps, seq.dtype)
        x = seq * jax.lax.rsqrt(jnp.mean(seq * seq, axis=-1, keepdims=True) + eps) * g_norm
        qkv = x @ W_qkv
        q, k, v = jnp.split(qkv, 3, axis=-1)

        def split_heads(t):
            return t.reshape(b, n_tot, HEADS, dh).transpose(0, 2, 1, 3)
        q, k, v = map(split_heads, (q, k, v))
        pos = jnp.arange(n_tot, dtype=seq.dtype)
        inv_freq = 1.0 / THETA ** (jnp.arange(0, dh, 2, dtype=seq.dtype) / dh)
        ang = jnp.repeat(pos[:, None] * inv_freq, 2, axis=-1)
        cos, sin = (jnp.cos(ang), jnp.sin(ang))
        q = q * cos + _rotate_half(q) * sin
        k = k * cos + _rotate_half(k) * sin
        w = n_tot // SEG

        def seg_fold(t):
            return t.reshape(b, HEADS, w, SEG, dh).transpose(0, 2, 1, 3, 4).reshape(b * w, HEADS, SEG, dh)
        q, k, v = map(seg_fold, (q, k, v))
        pmk = jnp.broadcast_to(pm[0], (b * w, HEADS, p, dh))
        pmv = jnp.broadcast_to(pm[1], (b * w, HEADS, p, dh))
        k = jnp.concatenate((pmk, k), axis=-2)
        v = jnp.concatenate((pmv, v), axis=-2)
        scores = jnp.einsum('bhid,bhjd->bhij', q, k) * dh ** (-0.5)
        i = jnp.arange(SEG)[:, None]
        j = jnp.arange(SEG + p)[None, :]
        mask = (j < p) | (j - p <= i)
        scores = jnp.where(mask, scores, NEG_INF)
        attn = jax.nn.softmax(scores, axis=-1)
        out = jnp.einsum('bhij,bhjd->bhid', attn, v)
        out = out.transpose(0, 2, 1, 3).reshape(b * w, SEG, HEADS * dh)
        out = out @ W_out
        return out.reshape(b, n_tot, dim)

    def _L0_ffn_ref(x, shared_w1, shared_w2, experts_w1, experts_w2, gate_w):
        import jax, jax.numpy as jnp
        import numpy as np
        D_MODEL = 128
        N_EXPERTS = 8
        TOP_K = 2
        HIDDEN = 4 * D_MODEL
        B, S, D = x.shape
        T = B * S
        x_flat = x.reshape(T, D)
        shared = jnp.einsum('td,dh->th', x_flat, shared_w1.T)
        shared = jnp.einsum('th,hd->td', jax.nn.silu(shared), shared_w2.T)
        gate_logits = x_flat @ gate_w.T
        top_k_gates, top_k_idx = jax.lax.top_k(gate_logits, TOP_K)
        top_k_gates = jax.nn.softmax(top_k_gates, axis=1)
        gates = jnp.zeros((T, N_EXPERTS), dtype=x.dtype)
        gates = gates.at[jnp.arange(T)[:, None], top_k_idx].set(top_k_gates)
        h = jnp.einsum('td,ehd->teh', x_flat, experts_w1)
        expert_out = jnp.einsum('teh,edh->ted', jax.nn.silu(h), experts_w2)
        selected = jnp.einsum('ted,te->td', expert_out, gates)
        return (shared + selected).reshape(B, S, D)
    x = L0_attn_seq
    x = x + 0.5 * _L0_ffn_ref(_layernorm(x, axis=-1), L0_ffn_shared_w1, L0_ffn_shared_w2, L0_ffn_experts_w1, L0_ffn_experts_w2, L0_ffn_gate_w)
    x = x + _L0_attn_ref(_layernorm(x, axis=-1), L0_attn_g_norm, L0_attn_W_qkv, L0_attn_W_out, L0_attn_pm)
    x = x + 0.5 * _L0_ffn_ref(_layernorm(x, axis=-1), L0_ffn_shared_w1, L0_ffn_shared_w2, L0_ffn_experts_w1, L0_ffn_experts_w2, L0_ffn_gate_w)
    return x

_drawn_inputs = setup_inputs


def setup_inputs(seed=0):
    import zlib

    import numpy as np

    out = dict(_drawn_inputs(seed))
    spreads = {'L0_attn_g_norm': (1.0, 0.2)}
    factors = {'L0_attn_pm': 31.897}
    for name, (base, spread) in spreads.items():
        noise = np.random.default_rng([zlib.crc32(name.encode()), seed]).standard_normal(out[name].shape)
        drawn = base * np.exp(spread * noise) if base else spread * noise
        out[name] = jnp.asarray(drawn.astype(out[name].dtype))
    for name, factor in factors.items():
        out[name] = (out[name] * factor).astype(out[name].dtype)
    return out
```

```python
from contextlib import ExitStack

import concourse.bass as bass
from concourse import mybir

F32 = mybir.dt.float32
F32R = mybir.dt.float32r
BF16 = mybir.dt.bfloat16
ALU = mybir.AluOpType
ACT = mybir.ActivationFunctionType
AX_X = mybir.AxisListType.X

P = 128
N = 512
NT = N // P
HEADS, DH, SEG, PM = 16, 64, 64, 16
HP = HEADS // 2
PAIRS = HP * NT
KEYS = P + PM
OWN = (0, P + 2 * PM)
PERSISTENT = slice(P, P + 2 * PM)
EXPERTS = 8
FE = 1 + EXPERTS
FJ = 4
FC = FE * FJ
LN_EPS = 1e-5
RMS_EPS = 2.0 ** -23
MASKED = -1e30

QK_COLS = 3 * DH
Q_AT = 2 * FE
K_AT = Q_AT + HP * QK_COLS // N
V_AT = K_AT + HP * QK_COLS // N
OUT_AT = V_AT + 2
BLOCKS = OUT_AT + 2
STAGES = 8

LAG = 3
SR = 4
HR = 3
PR = 3
LEAD = 6
UNITS = 4 * HP
T_LAG, AV_LAG = 2, 3
O_LAG = NT - 1 + AV_LAG
W_LAG = O_LAG + 2
SLOTS = NT * (HP - 1) + W_LAG + 1


def macaron(nc, x_in, weights, gate_w, g_norm, pm_k, pm_v, rotary, x_out):
    groups = x_in.shape[0] - 1
    ctx = ExitStack()
    with ctx:
        def sb(name, shape, dt=F32):
            return ctx.enter_context(nc.sbuf_tensor(name, shape, dt))

        def sem(name):
            return ctx.enter_context(nc.semaphore(name))

        w_hi = sb("w_hi", [P, BLOCKS * N], F32R)
        w_lo = sb("w_lo", [P, BLOCKS * N], F32R)
        values = sb("values", [P, NT, HEADS * DH])
        k_diag = [sb(f"k_diag{i}", [P, NT, 2 * KEYS]) for i in range(2)]
        hidden = sb("hidden", [P, SR, N])
        h_hi = sb("h_hi", [P, HR, N], F32R)
        h_lo = sb("h_lo", [P, HR, N], F32R)
        scratch = sb("scratch", [P, 4 * N])
        gate_cols = [scratch[:, i * N:(i + 1) * N] for i in range(2)]
        gated = [scratch[:, (2 + i) * N:(3 + i) * N] for i in range(2)]
        q_rot = [scratch[:, i * N:(i + 1) * N] for i in range(2)]
        probs = [scratch[:, 2 * N + i * 2 * KEYS:2 * N + (i + 1) * 2 * KEYS]
                 for i in range(PR)]
        probs_t = sb("probs_t", [P, 2, 2 * P])
        pm_t = sb("pm_t", [96, N], F32R)
        norm_hi = [sb(f"norm_hi{i}", [P, N], F32R) for i in range(3)]
        norm_lo = [sb(f"norm_lo{i}", [P, N], F32R) for i in range(3)]
        gates_t = [sb(f"gates_t{i}", [DH, N], F32R) for i in range(2)]
        x1 = sb("x1", [P, NT, P])
        x2 = sb("x2", [P, NT, P])
        x3 = sb("x3", [P, NT, P])
        x_hat = sb("x_hat", [P, NT, P])
        acc = sb("acc", [P, N])
        tables = sb("tables", [P, 4, N // 2])
        ident = sb("ident", [P, P])
        ident_bf = sb("ident_bf", [P, P], BF16)
        mask_bf = sb("mask_bf", [P, 2 * KEYS], BF16)
        gate_raw = sb("gate_raw", [P, EXPERTS])
        gate_hi = sb("gate_hi", [P, EXPERTS], F32R)
        gate_lo = sb("gate_lo", [P, EXPERTS], F32R)
        pick_raw = sb("pick_raw", [DH, EXPERTS])
        pick = sb("pick", [DH, EXPERTS], F32R)
        below = sb("below", [P, EXPERTS, EXPERTS])
        above = sb("above", [P, EXPERTS, EXPERTS])
        head_rows = sb("head_rows", [P, 2])
        g_col = sb("g_col", [P, 1])
        pmk_sb = sb("pmk_sb", [P, HP, 2 * PM])
        pmv_sb = sb("pmv_sb", [96, HP, P], F32R)
        stats = sb("stats", [P, NT, 6])
        mean_var = sb("mean_var", [P, NT, 2])
        rstd = sb("rstd", [P, 4, NT])
        minus_half = sb("minus_half", [P, NT])
        logits = sb("logits", [P, NT, EXPERTS])
        top8 = sb("top8", [P, NT, EXPERTS])
        cmp_ge, cmp_gt = (x_hat[:, i:i + NT // 2, :].rearrange("p a (b e j) -> p (a b) e j", e=EXPERTS, j=EXPERTS)
                          for i in (0, NT // 2))
        rank = sb("rank", [P, NT, EXPERTS])
        top_sum = sb("top_sum", [P, NT, 1])
        centred = sb("centred", [P, NT, EXPERTS])
        tanhs = sb("tanhs", [P, NT, EXPERTS])
        gates = sb("gates", [P, NT, EXPERTS])
        neg_max = sb("neg_max", [P, 4, 2])
        row_sum = sb("row_sum", [P, 4, 2])
        row_inv = sb("row_inv", [P, 4, 2])

        bank = [ctx.enter_context(nc.psum_tensor(f"bank{i}", [P, N], F32)) for i in range(8)]
        side = bank[7]

        ld_x, ld_small, ld_pmv, st_out = sem("ld_x"), sem("ld_small"), sem("ld_pmv"), sem("st_out")
        ld_w = [sem(f"ld_w{i}") for i in range(STAGES)]
        split_hi, split_lo = sem("split_hi"), sem("split_lo")
        consts_pool, consts_act, consts_dve, pool_self = sem("consts_pool"), sem("consts_act"), sem("consts_dve"), sem("pool_self")
        hid_made, hid_silu, hid_hi_act, hid_hi_pool, hid_lo = (
            sem("hid_made"), sem("hid_silu"), sem("hid_hi_act"), sem("hid_hi_pool"), sem("hid_lo"))
        down_done, y_used, gcols_made, gcols_copied, acc_added = (
            sem("down_done"), sem("y_used"), sem("gcols_made"), sem("gcols_copied"), sem("acc_added"))
        side_made, side_used = sem("side_made"), sem("side_used")
        passed = sem("passed")
        stats_ready, rstd_ready, xhat_ready, norm_hi_ready = (
            sem("stats_ready"), sem("rstd_ready"), sem("xhat_ready"), sem("norm_hi_ready"))
        prep_self, norm_self, centred_ready, tanh_ready, gates_ready, gates_hi_ready = (
            sem("prep_self"), sem("norm_self"), sem("centred_ready"), sem("tanh_ready"), sem("gates_ready"), sem("gates_hi_ready"))
        v_made, v_copied, proj_made, rot_mul, q_ready, k_ready, k_added, rstd_self = (
            sem("v_made"), sem("v_copied"), sem("proj_made"), sem("rot_mul"), sem("q_ready"), sem("k_ready"),
            sem("k_added"), sem("rstd_self"))
        s_made, max_ready, exp_done, inv_ready, p_ready = (
            sem("s_made"), sem("max_ready"), sem("exp_done"), sem("inv_ready"), sem("p_ready"))
        t_made, pmt_hi, t_copied, pmt_lo, av_done = (
            sem("t_made"), sem("pmt_hi"), sem("t_copied"), sem("pmt_lo"), sem("av_done"))
        o_hi, o_lo, wout_done, yatt_copied = sem("o_hi"), sem("o_lo"), sem("wout_done"), sem("yatt_copied")

        def w1(part, e, j):
            return part[:, 2 * e * N + j * P:2 * e * N + (j + 1) * P]

        def w2(part, e, j):
            return part[:, (2 * e + 1) * N + j * P:(2 * e + 1) * N + (j + 1) * P]

        def wait(eng, s, value):
            if not isinstance(value, int) or value > 0:
                eng.wait_ge(s, value)

        def wait_apart(eng, *waits):
            for s, v in waits:
                wait(eng, s, v)
            eng.sem_inc(passed, 1)

        def program(eng, ffn, attention, prep, finish, start):
            start()
            prep(None, role=0, n=0, r=0, m=0, src=x1, loads=1)
            ffn(None, f=0, role=0, m=0, first=True)
            finish(None, role=0, m=3, count=0, g=0)
            prep(None, role=1, n=1, r=None, m=4, src=x2)

            def beside_first_attention(slot):
                prep(slot - 4, role=0, n=2, r=1, m=5, src=x1, loads=2)
            attention(a=0, m=4, beside=beside_first_attention)

            with eng.Fori(0, groups - 1) as g:
                def beside_first_ffn(slot):
                    finish(slot - 1, role=1, m=10 * g + 8, count=g, g=g)
                    prep(slot - 5, role=2, n=3 * g + 3, r=2 * g + 2, m=10 * g + 9, src=x3)
                ffn(beside_first_ffn, f=2 * g + 1, role=0, m=10 * g + 5, first=False)

                def beside_second_ffn(slot):
                    finish(slot - 2, role=0, m=10 * g + 12, count=2 * g + 1, g=g)
                    prep(slot - 6, role=1, n=3 * g + 4, r=None, m=10 * g + 13, src=x2)
                ffn(beside_second_ffn, f=2 * g + 2, role=2, m=10 * g + 9, first=False)

                def beside_attention(slot):
                    finish(slot - 0, role=2, m=10 * g + 14, count=2 * g + 2, g=g)
                    prep(slot - 4, role=0, n=3 * g + 5, r=2 * g + 3, m=10 * g + 15, src=x1, loads=g + 3)
                attention(a=g + 1, m=10 * g + 13, beside=beside_attention)

            g = groups - 1
            finish(None, role=1, m=10 * g + 8, count=g, g=g)
            prep(None, role=2, n=3 * g + 3, r=2 * g + 2, m=10 * g + 9, src=x3)
            ffn(None, f=2 * g + 1, role=2, m=10 * g + 9, first=False)
            finish(None, role=2, m=10 * g + 12, count=2 * g + 1, g=g)

        def steps_of(slot, steps):
            return range(steps) if slot is None else [slot] if 0 <= slot < steps else []

        PREP = 12

        block = ctx.enter_context(nc.Block())

        @block.sync
        def _(sp):
            sp.sem_inc(st_out, 16)
            sp.dma_start(x1[:], x_in[0]).then_inc(ld_x, 16)
            for dst, src in ((gate_raw[:], gate_w), (g_col[:], g_norm), (pmk_sb[:], pm_k), (tables[:], rotary)):
                sp.dma_start(dst, src).then_inc(ld_small, 16)
            sp.dma_start(x_hat_stage(values), pm_v).then_inc(ld_pmv, 16)
            for b, blk in enumerate(split_order()):
                slot = b % (STAGES - 2)
                if b >= STAGES - 2:
                    sp.wait_ge(split_lo, b - (STAGES - 2) + 1)
                sp.dma_start(stage(values, slot), weights[:, blk * N:(blk + 1) * N]).then_inc(ld_w[slot], 16)
            sp.wait_ge(side_used, 4)
            sp.dma_start(x1[:], x_in[1]).then_inc(ld_x, 16)
            with sp.Fori(0, groups - 1) as g:
                wait_apart(sp, (side_used, 10 * g + 13))
                sp.dma_start(x1[:], x_in[2:][g]).then_inc(ld_x, 16)
                wait_apart(sp, (side_used, 10 * g + 15))
                sp.dma_start(x_out[g], x3[:]).then_inc(st_out, 16)
            sp.wait_ge(side_used, 10 * (groups - 1) + 13)
            sp.dma_start(x_out[groups - 1], x3[:]).then_inc(st_out, 16)
            sp.wait_ge(st_out, 16 * (groups + 1))
            sp.wait_ge(ld_x, 16 * (groups + 1))

        @block.tensor
        def _(pe):
            def split3(out, lhs_hi, lhs_lo, rhs_hi, rhs_lo, start, stop):
                nc.tensor.matmul(out, lhs_hi, rhs_hi, start=start, stop=False)
                nc.tensor.matmul(out, lhs_hi, rhs_lo, start=False, stop=False)
                return nc.tensor.matmul(out, lhs_lo, rhs_hi, start=False, stop=stop)

            def start():
                pe.wait_ge(consts_pool, 1)
                pe.wait_ge(consts_dve, 1)

            def ffn(beside, f, role, m, first):
                for c in range(FC + LAG):
                    if c < FC:
                        e, j = divmod(c, FJ)
                        if c == 0:
                            pe.wait_ge(side_used, m + 1)
                        if first and j == 0:
                            pe.wait_ge(split_lo, blocks_before(e + 1))
                        if j == 0 and e >= 1:
                            if e == 1:
                                pe.wait_ge(side_used, m + 3)
                            wait(pe, gcols_copied, EXPERTS * f + e - 1)
                            nc.tensor.matmul(bank[6][:], pick[:, e - 1:e].broadcast_to([DH, P]),
                                             gates_t[role // 2][:], start=True, stop=True).then_inc(gcols_made, 1)
                        wait(pe, hid_silu, FC * f + c - 3)
                        split3(bank[c % 4][:], w1(w_hi, e, j), w1(w_lo, e, j), norm_hi[role][:],
                               norm_lo[role][:], True, True).then_inc(hid_made, 1)
                    if c >= LAG:
                        d = c - LAG
                        e, j = divmod(d, FJ)
                        if j == 0:
                            wait(pe, y_used, FE * f + max(e - 1, 0))
                        pe.wait_ge(hid_lo, FC * f + d + 1)
                        split3(bank[4 + e % 2][:], w2(w_hi, e, j), w2(w_lo, e, j), h_hi[:, d % HR, :],
                               h_lo[:, d % HR, :], j == 0, j == FJ - 1).then_inc(down_done, 1)
                    if beside:
                        beside(c)

            def attention(a, m, beside):
                xh, xl = norm_hi[1], norm_lo[1]
                pe.wait_ge(side_used, m + 1)
                if isinstance(a, int):
                    pe.wait_ge(split_lo, BLOCKS)
                for v in range(2 * NT):
                    t, half = divmod(v, 2)
                    if v >= 2:
                        pe.wait_ge(v_copied, 2 * NT * a + v - 1)
                    cols = slice((V_AT + half) * N, (V_AT + half + 1) * N)
                    rows = slice(t * P, (t + 1) * P)
                    split3(bank[v % 2][:], xh[:, rows], xl[:, rows], w_hi[:, cols], w_lo[:, cols],
                           True, True).then_inc(v_made, 1)

                def project(w):
                    hp, j = divmod(w, 4)
                    if w < 2:
                        pe.wait_ge(v_copied, 2 * NT * a + 2 * NT)
                    else:
                        pe.wait_ge(rot_mul, UNITS * a + w - 1)
                    at = (Q_AT, K_AT)[j // 2] * N + hp * QK_COLS + j % 2 * DH
                    parts = [x[:, at:at + P] for x in (w_hi, w_lo)]
                    split3(bank[w % 2][:], *parts, xh[:], xl[:], True, True).then_inc(proj_made, 1)

                def scores(s):
                    hp, p = divmod(s, NT)
                    if p == 0:
                        pe.wait_ge(q_ready, HP * a + hp + 1)
                        pe.wait_ge(k_ready, HP * a + hp + 1)
                    if s >= 2:
                        pe.wait_ge(exp_done, 2 * (PAIRS * a + s - 1))
                    out = bank[2 + s % 2][:, 0:2 * KEYS]
                    nc.tensor.matmul(out, ident_bf[:], mask_bf[:], start=True, stop=False)
                    nc.tensor.matmul(out, q_rot[hp % 2][:, p * P:(p + 1) * P],
                                     k_diag[hp % 2][:, p], start=False, stop=True).then_inc(s_made, 1)

                def transpose(s):
                    pe.wait_ge(p_ready, PAIRS * a + s + 1)
                    if s >= 1:
                        pe.wait_ge(pmt_lo, PAIRS * a + s)
                    for h in range(2):
                        nc.tensor.transpose(bank[4][:, h * P:(h + 1) * P], probs[s % PR][:, OWN[h]:OWN[h] + P], ident[:])
                    nc.tensor.transpose(bank[4][0:2 * PM, 2 * P:3 * P], probs[s % PR][:, PERSISTENT],
                                        ident[:]).then_inc(t_made, 1)

                def weigh_values(s):
                    hp, p = divmod(s, NT)
                    pe.wait_ge(t_copied, PAIRS * a + s + 1)
                    if p == 0 and hp >= 1:
                        pe.wait_ge(o_lo, HP * a + hp)
                    for h in range(2):
                        head = slice((2 * hp + h) * DH, (2 * hp + h + 1) * DH)
                        last = nc.tensor.matmul(bank[5][h * DH:(h + 1) * DH, p * P:(p + 1) * P],
                                                values[:, p, head], probs_t[:, s % 2, h * P:(h + 1) * P],
                                                start=p == 0, stop=False, skip_group_check=True)
                    if p == NT - 1:
                        pe.wait_ge(pmt_lo, PAIRS * a + s + 1)
                        last = nc.tensor.matmul(bank[5][:], pmv_sb[:, hp, :], pm_t[:],
                                                start=False, stop=True, skip_group_check=True)
                    last.then_inc(av_done, 1)

                def times_w_out(hp):
                    pe.wait_ge(o_lo, HP * a + hp + 1)
                    cols = slice(OUT_AT * N + hp * P, OUT_AT * N + (hp + 1) * P)
                    split3(bank[6][:], w_hi[:, cols], w_lo[:, cols], h_hi[:, hp % 2, :], h_lo[:, hp % 2, :],
                           hp == 0, hp == HP - 1).then_inc(wout_done, 1)

                for w in range(LEAD):
                    project(w)
                for s in range(SLOTS):
                    if s < PAIRS:
                        scores(s)
                    if s + LEAD < UNITS:
                        project(s + LEAD)
                    if 0 <= s - T_LAG < PAIRS:
                        transpose(s - T_LAG)
                    if 0 <= s - AV_LAG < PAIRS:
                        weigh_values(s - AV_LAG)
                    if s >= W_LAG and (s - W_LAG) % NT == 0:
                        times_w_out((s - W_LAG) // NT)
                    beside(s)

            def prep(slot, role, n, r, m, src, loads=None):
                for step in steps_of(slot, PREP):
                    if step == 3:
                        pe.wait_ge(xhat_ready, n + 1)
                        wait(pe, side_used, m)
                        for t in range(NT):
                            last = nc.tensor.transpose(side[:, t * P:(t + 1) * P], x_hat[:, t, :], ident[:])
                        last.then_inc(side_made, 1)
                    if step == 5 and role != 1:
                        pe.wait_ge(side_used, m + 1)
                        for t in range(NT):
                            rows = slice(t * P, (t + 1) * P)
                            last = split3(side[:, t * EXPERTS:(t + 1) * EXPERTS], norm_hi[role][:, rows],
                                          norm_lo[role][:, rows], gate_hi[:], gate_lo[:], True, True)
                        last.then_inc(side_made, 1)
                    if step == 10 and role != 1:
                        pe.wait_ge(gates_ready, r + 1)
                        pe.wait_ge(side_used, m + 2)
                        for t in range(NT):
                            last = nc.tensor.transpose(side[0:EXPERTS, t * P:(t + 1) * P], gates[:, t, :], ident[:])
                        last.then_inc(side_made, 1)

            def finish(slot, role, m, count, g):
                for step in steps_of(slot, 3):
                    if step == 1:
                        if role == 1:
                            pe.wait_ge(yatt_copied, count + 1)
                        else:
                            pe.wait_ge(acc_added, EXPERTS * (count + 1))
                        pe.wait_ge(side_used, m)
                        for t in range(NT):
                            last = nc.tensor.transpose(side[:, t * P:(t + 1) * P], acc[:, t * P:(t + 1) * P], ident[:])
                        last.then_inc(side_made, 1)

            program(nc.tensor, ffn, attention, prep, finish, start)

        @block.scalar
        def _(act):
            def split_block(b, blk):
                slot = b % (STAGES - 2)
                act.wait_ge(ld_w[slot], 16 * (b // (STAGES - 2) + 1))
                nc.scalar.activation(w_hi[:, blk * N:(blk + 1) * N], stage(values, slot), ACT.Copy).then_inc(split_hi, 1)

            order = split_order()

            def start():
                act.wait_ge(ld_small, 16 * 4)
                nc.scalar.activation(gate_hi[:], gate_raw[:], ACT.Copy)
                act.wait_ge(consts_pool, 2)
                nc.scalar.activation(pick[:], pick_raw[:], ACT.Copy)
                act.wait_ge(ld_pmv, 16)
                nc.scalar.activation(pmv_sb[:], x_hat_stage(values), ACT.Copy).then_inc(consts_act, 1)
                for b in range(blocks_before(1)):
                    split_block(b, order[b])

            def ffn(beside, f, role, m, first):
                for c in range(FC + LAG):
                    if first and c % FJ == 0 and c < FC:
                        e = c // FJ
                        for b in range(blocks_before(e + 1), blocks_before(e + 2)):
                            split_block(b, order[b])
                    if c < FC:
                        act.wait_ge(hid_made, FC * f + c + 1)
                        wait(act, hid_lo, FC * f + c - SR + 1)
                        nc.scalar.activation(hidden[:, c % SR, :], bank[c % 4][:], ACT.Silu).then_inc(hid_silu, 1)
                    d = c - 1
                    if 0 <= d < FC and d % 2 == 1:
                        act.wait_ge(hid_silu, FC * f + d + 1)
                        wait(act, down_done, FC * f + d - HR + 1)
                        nc.scalar.activation(h_hi[:, d % HR, :], hidden[:, d % SR, :], ACT.Copy).then_inc(hid_hi_act, 1)
                    if c % FJ == 0 and 1 <= c // FJ < FE:
                        e = c // FJ
                        act.wait_ge(gcols_made, EXPERTS * f + e)
                        wait(act, y_used, FE * f + e - 1)
                        nc.scalar.activation(gate_cols[e % 2], bank[6][:], ACT.Copy).then_inc(gcols_copied, 1)
                    if beside:
                        beside(c)

            def attention(a, m, beside):
                for v in range(2 * NT):
                    t, half = divmod(v, 2)
                    act.wait_ge(v_made, 2 * NT * a + v + 1)
                    nc.scalar.activation(values[:, t, half * N:(half + 1) * N], bank[v % 2][:],
                                         ACT.Copy).then_inc(v_copied, 1)

                def exps(s):
                    act.wait_ge(max_ready, PAIRS * a + s + 1)
                    if s >= PR:
                        act.wait_ge(t_made, PAIRS * a + s - PR + 1)
                    for h in range(2):
                        nc.scalar.activation(probs[s % PR][:, h * KEYS:(h + 1) * KEYS], bank[2 + s % 2][:, h * KEYS:(h + 1) * KEYS],
                                             ACT.Exp, bias=neg_max[:, s % 4, h:h + 1],
                                             accum_out=row_sum[:, s % 4, h:h + 1]).then_inc(exp_done, 1)

                def copy_transposed(s):
                    hp, p = divmod(s, NT)
                    act.wait_ge(t_made, PAIRS * a + s + 1)
                    if p == 0 and hp >= 1:
                        act.wait_ge(av_done, PAIRS * a + s)
                    elif s >= 2:
                        act.wait_ge(av_done, PAIRS * a + s - 1)
                    tok = slice(p * P, (p + 1) * P)
                    pm_part = bank[4][0:2 * PM, 2 * P:3 * P]
                    nc.scalar.activation(pm_t[0:32, tok], pm_part, ACT.Copy)
                    nc.scalar.activation(pm_t[64:96, tok], pm_part, ACT.Copy)
                    nc.scalar.activation(probs_t[:, s % 2, :], bank[4][:, 0:2 * P], ACT.Copy).then_inc(t_copied, 1)

                def output_hi(hp):
                    act.wait_ge(av_done, PAIRS * a + NT * (hp + 1))
                    if hp >= 2:
                        act.wait_ge(wout_done, HP * a + hp - 1)
                    nc.scalar.activation(h_hi[:, hp % 2, :], bank[5][:], ACT.Copy).then_inc(o_hi, 1)

                for s in range(SLOTS):
                    if s < PAIRS:
                        exps(s)
                    if 0 <= s - T_LAG < PAIRS:
                        copy_transposed(s - T_LAG)
                    if s >= O_LAG and (s - O_LAG) % NT == 0 and (s - O_LAG) // NT < HP:
                        output_hi((s - O_LAG) // NT)
                    beside(s)
                act.wait_ge(wout_done, HP * (a + 1))
                nc.scalar.activation(acc[:], bank[6][:], ACT.Copy).then_inc(yatt_copied, 1)

            def prep(slot, role, n, r, m, src, loads=None):
                for step in steps_of(slot, PREP):
                    if step == 4:
                        act.wait_ge(side_made, m + 1)
                        scale = g_col[:, 0:1] if role == 1 else 1.0
                        nc.scalar.activation(norm_hi[role][:], side[:], ACT.Copy, scale=scale).then_inc(norm_hi_ready, 1)
                    if step == 8 and role != 1:
                        act.wait_ge(centred_ready, r + 1)
                        nc.scalar.activation(tanhs[:], centred[:], ACT.Tanh).then_inc(tanh_ready, 1)
                    if step == 11 and role != 1:
                        act.wait_ge(side_made, m + 3)
                        nc.scalar.activation(gates_t[role // 2][0:EXPERTS, :], side[0:EXPERTS, :],
                                             ACT.Copy).then_inc(gates_hi_ready, 1)

            def finish(slot, role, m, count, g):
                pass

            program(nc.scalar, ffn, attention, prep, finish, start)

        @block.vector
        def _(dve):
            order = split_order()

            def split_block(b, blk):
                slot = b % (STAGES - 2)
                dve.wait_ge(split_hi, b + 1)
                cols = slice(blk * N, (blk + 1) * N)
                nc.vector.tensor_tensor(w_lo[:, cols], stage(values, slot), w_hi[:, cols].bitcast(F32),
                                        ALU.subtract).then_inc(split_lo, 1)

            def start():
                dve.wait_ge(consts_act, 1)
                nc.vector.tensor_tensor(gate_lo[:], gate_raw[:], gate_hi[:].bitcast(F32), ALU.subtract)
                low = slice(64, 96)
                nc.vector.tensor_tensor(pmv_sb[low], x_hat_stage(values)[low], pmv_sb[low].bitcast(F32),
                                        ALU.subtract).then_inc(consts_dve, 1)
                dve.wait_ge(consts_pool, 3)

            def ffn(beside, f, role, m, first):
                if first:
                    for b in range(blocks_before(1)):
                        split_block(b, order[b])

                def use_output(e):
                    dve.wait_ge(down_done, FC * f + FJ * (e + 1))
                    y = bank[4 + e % 2][:]
                    if e == 0:
                        nc.vector.tensor_scalar(acc[:], y, 0.5, None, ALU.mult).then_inc(y_used, 1)
                    else:
                        dve.wait_ge(gcols_copied, EXPERTS * f + e)
                        if e >= 3:
                            dve.wait_ge(acc_added, EXPERTS * f + e - 2)
                        nc.vector.tensor_tensor(gated[e % 2], y, gate_cols[e % 2], ALU.mult).then_inc(y_used, 1)

                for c in range(FC + LAG):
                    if first and c % FJ == 0 and c < FC:
                        e = c // FJ
                        for b in range(blocks_before(e + 1), blocks_before(e + 2)):
                            split_block(b, order[b])
                    if c < FC:
                        dve.wait_ge(hid_silu, FC * f + c + 1)
                        if c % 2:
                            dve.wait_ge(hid_hi_act, FC // 2 * f + c // 2 + 1)
                        else:
                            dve.wait_ge(hid_hi_pool, FC // 2 * f + c // 2 + 1)
                        wait(dve, down_done, FC * f + c - HR + 1)
                        nc.vector.tensor_tensor(h_lo[:, c % HR, :], hidden[:, c % SR, :],
                                                h_hi[:, c % HR, :].bitcast(F32), ALU.subtract).then_inc(hid_lo, 1)
                    if c >= FJ - 1 + LAG and (c - LAG) % FJ == FJ - 1:
                        use_output((c - LAG) // FJ)
                    if beside:
                        beside(c)

            def attention(a, m, beside):
                def rotate(w):
                    hp, j = divmod(w, 4)
                    dve.wait_ge(proj_made, UNITS * a + w + 1)
                    if j == 0:
                        wait(dve, q_ready, HP * a + hp)
                    if j == 2:
                        wait(dve, k_ready, HP * a + hp)
                    table = tables[:, j:j + 1, :].broadcast_to([P, 2, N // 2])
                    nc.vector.tensor_tensor(hidden[:, j, :].rearrange("p (b n) -> p b n", b=2),
                                            bank[w % 2][:].rearrange("p (b n) -> p b n", b=2), table,
                                            ALU.mult).then_inc(rot_mul, 1)

                def find_max(s):
                    dve.wait_ge(s_made, PAIRS * a + s + 1)
                    nc.vector.tensor_reduce(neg_max[:, s % 4, :], bank[2 + s % 2][:, 0:2 * KEYS].rearrange(
                        "p (h k) -> p h k", h=2), AX_X, ALU.max, negate=True).then_inc(max_ready, 1)

                def normalise(s):
                    dve.wait_ge(exp_done, 2 * (PAIRS * a + s + 1))
                    nc.vector.reciprocal(row_inv[:, s % 4, :], row_sum[:, s % 4, :]).then_inc(inv_ready, 1)
                    dve.wait_ge(inv_ready, PAIRS * a + s + 1)
                    part = probs[s % PR]
                    for h in range(2):
                        last = nc.vector.tensor_scalar(part[:, h * KEYS:(h + 1) * KEYS], part[:, h * KEYS:(h + 1) * KEYS],
                                                       row_inv[:, s % 4, h:h + 1], None, ALU.mult)
                    last.then_inc(p_ready, 1)

                def pm_low(s):
                    hp, p = divmod(s, NT)
                    dve.wait_ge(t_copied, PAIRS * a + s + 1)
                    tok = slice(p * P, (p + 1) * P)
                    nc.vector.tensor_tensor(pm_t[32:64, tok], bank[4][0:32, 2 * P:3 * P],
                                            pm_t[0:32, tok].bitcast(F32), ALU.subtract).then_inc(pmt_lo, 1)

                def output_low(hp):
                    dve.wait_ge(o_hi, HP * a + hp + 1)
                    nc.vector.tensor_tensor(h_lo[:, hp % 2, :], bank[5][:], h_hi[:, hp % 2, :].bitcast(F32),
                                            ALU.subtract).then_inc(o_lo, 1)

                for w in range(LEAD):
                    rotate(w)
                for s in range(SLOTS):
                    if s < PAIRS:
                        find_max(s)
                    if 0 <= s - 1 < PAIRS:
                        normalise(s - 1)
                    if s + LEAD < UNITS:
                        rotate(s + LEAD)
                    if 0 <= s - T_LAG < PAIRS:
                        pm_low(s - T_LAG)
                    if s >= O_LAG and (s - O_LAG) % NT == 0 and (s - O_LAG) // NT < HP:
                        output_low((s - O_LAG) // NT)
                    beside(s)

            LINKS = 9

            def prep(slot, role, n, r, m, src, loads=None):
                for step in steps_of(slot, PREP):
                    if step == 0:
                        if role == 0:
                            dve.wait_ge(ld_x, 16 * loads)
                        else:
                            dve.wait_ge(side_used, m)
                        for t in range(NT):
                            last = nc.vector.bn_stats(stats[:, t, :], src[:, t, :])
                        last.then_inc(norm_self, 1)
                        wait_apart(dve, (norm_self, n + 1))
                        for t in range(NT):
                            last = nc.vector.bn_aggr(mean_var[:, t, :], stats[:, t, :])
                        last.then_inc(stats_ready, 1)
                    if step == 2:
                        dve.wait_ge(rstd_ready, n + 1)
                        scale = 3 if role == 1 else 1
                        for t in range(NT):
                            last = nc.vector.tensor_scalar(x_hat[:, t, :], src[:, t, :], mean_var[:, t, 0:1],
                                                           rstd[:, scale, t:t + 1], ALU.subtract, ALU.mult)
                        last.then_inc(xhat_ready, 1)
                    if step == 4:
                        dve.wait_ge(norm_hi_ready, n + 1)
                        high = norm_hi[role][:].bitcast(F32)
                        if role == 1:
                            nc.vector.scalar_tensor_tensor(norm_lo[role][:], side[:], g_col[:, 0:1], high,
                                                           ALU.mult, ALU.subtract).then_inc(side_used, 1)
                        else:
                            nc.vector.tensor_tensor(norm_lo[role][:], side[:], high, ALU.subtract).then_inc(side_used, 1)
                    if role == 1:
                        continue
                    if step == 6:
                        done = [0]

                        def link(ins):
                            done[0] += 1
                            ins.then_inc(prep_self, 1)
                            dve.wait_ge(prep_self, LINKS * r + done[0])
                        dve.wait_ge(side_made, m + 2)
                        nc.vector.tensor_copy(logits[:], side[:, 0:NT * EXPERTS].rearrange(
                            "p (t e) -> p t e", t=NT)).then_inc(side_used, 1)
                        wait_apart(dve, (side_used, m + 2))
                        other = logits[:].unsqueeze(2).broadcast_to([P, NT, EXPERTS, EXPERTS])
                        own = logits[:].unsqueeze(3).broadcast_to([P, NT, EXPERTS, EXPERTS])
                        for t in range(NT):
                            last = nc.vector.max(top8[:, t, :], logits[:, t, :])
                        link(last)
                        link(nc.vector.tensor_tensor(cmp_ge, other, own, ALU.is_ge))
                        link(nc.vector.tensor_tensor(cmp_gt, other, own, ALU.is_gt))
                        tie = below[:].unsqueeze(1).broadcast_to([P, NT, EXPERTS, EXPERTS])
                        rest = above[:].unsqueeze(1).broadcast_to([P, NT, EXPERTS, EXPERTS])
                        link(nc.vector.tensor_tensor(cmp_ge, cmp_ge, tie, ALU.mult))
                        link(nc.vector.tensor_tensor(cmp_gt, cmp_gt, rest, ALU.mult))
                        link(nc.vector.tensor_tensor(cmp_gt, cmp_gt, cmp_ge, ALU.add))
                        link(nc.vector.tensor_reduce(rank[:], cmp_gt, AX_X, ALU.add))
                        link(nc.vector.tensor_scalar(rank[:], rank[:], 2.0, 0.25, ALU.is_lt, ALU.mult))
                        link(nc.vector.tensor_tensor(top_sum[:], top8[:, :, 0:1], top8[:, :, 1:2], ALU.add))
                        nc.vector.scalar_tensor_tensor(centred[:], top_sum[:].broadcast_to([P, NT, EXPERTS]), -0.5,
                                                       logits[:], ALU.mult, ALU.add).then_inc(centred_ready, 1)
                        assert done[0] == LINKS
                    if step == 9:
                        dve.wait_ge(tanh_ready, r + 1)
                        nc.vector.scalar_tensor_tensor(gates[:], tanhs[:], 1.0, rank[:], ALU.add,
                                                       ALU.mult).then_inc(gates_ready, 1)
                    if step == 11:
                        dve.wait_ge(gates_hi_ready, r + 1)
                        part = gates_t[role // 2]
                        nc.vector.tensor_tensor(part[32:32 + EXPERTS, :], side[0:EXPERTS, :],
                                                part[0:EXPERTS, :].bitcast(F32), ALU.subtract).then_inc(side_used, 1)

            def finish(slot, role, m, count, g):
                for step in steps_of(slot, 3):
                    if step == 2:
                        dve.wait_ge(side_made, m + 1)
                        old, new = ((x1, x2), (x2, x3), (x3, x3))[role]
                        if role == 1:
                            wait(dve, st_out, 16 * g + 16)
                        nc.vector.tensor_tensor(new[:], side[:].rearrange("p (t d) -> p t d", t=NT), old[:],
                                                ALU.add).then_inc(side_used, 1)

            program(nc.vector, ffn, attention, prep, finish, start)

        @block.gpsimd
        def _(pool):
            def start():
                done = [0]

                def link(ins):
                    done[0] += 1
                    ins.then_inc(pool_self, 1)
                    pool.wait_ge(pool_self, done[0])

                link(nc.gpsimd.memset(ident[:], 0.0))
                link(nc.gpsimd.memset(ident_bf[:], 0.0))
                link(nc.gpsimd.memset(mask_bf[:], 0.0))
                link(nc.gpsimd.memset(pick_raw[:], 0.0))
                for x in (ident, ident_bf):
                    link(nc.gpsimd.affine_select(out=x[:], in_=x[:], compare_op=ALU.not_equal, fill=1.0, base=0,
                                                 pattern=[[-1, P]], channel_multiplier=1))
                for at in OWN:
                    own = mask_bf[:, at:at + P]
                    link(nc.gpsimd.affine_select(out=own, in_=own, compare_op=ALU.is_ge, fill=MASKED, base=0,
                                                 pattern=[[-1, P]], channel_multiplier=1))
                    link(nc.gpsimd.memset(mask_bf[SEG:P, at:at + SEG], MASKED))
                pool.sem_inc(consts_pool, 1)
                for base in (0, -32):
                    last = nc.gpsimd.affine_select(out=pick_raw[:], in_=pick_raw[:], compare_op=ALU.not_equal,
                                                   fill=1.0, base=base, pattern=[[-1, EXPERTS]], channel_multiplier=1)
                    if base == 0:
                        link(last)
                last.then_inc(consts_pool, 1)
                nc.gpsimd.memset(minus_half[:], -0.5)
                for quarter, (first, second) in enumerate(((1.0, 0.0), (0.0, 1.0), (1.0, 0.0), (0.0, 1.0))):
                    rows = slice(quarter * 32, (quarter + 1) * 32)
                    link(nc.gpsimd.memset(head_rows[rows, 0:1], first))
                    link(nc.gpsimd.memset(head_rows[rows, 1:2], second))
                for i in range(2):
                    nc.gpsimd.memset(gates_t[i][:].bitcast(F32), 0.0)
                    nc.gpsimd.memset(k_diag[i][:], 0.0)
                nc.gpsimd.memset(below[:], 1.0)
                link(nc.gpsimd.memset(above[:], 1.0))
                for x, sign in ((below, 1), (above, -1)):
                    last = nc.gpsimd.affine_select(out=x[:], in_=x[:], compare_op=ALU.is_gt, fill=0.0, base=0,
                                                   pattern=[[sign, EXPERTS], [-sign, EXPERTS]], channel_multiplier=0)
                last.then_inc(consts_pool, 1)
                pool.wait_ge(consts_pool, 3)
                pool.wait_ge(ld_small, 16 * 4)

            def ffn(beside, f, role, m, first):
                def add_output(e):
                    pool.wait_ge(y_used, FE * f + e + 1)
                    if e >= 2:
                        pool.wait_ge(acc_added, EXPERTS * f + e - 1)
                    nc.gpsimd.tensor_tensor(acc[:], acc[:], gated[e % 2], ALU.add).then_inc(acc_added, 1)

                for c in range(FC + LAG + 1):
                    if c < FC and c % 2 == 0:
                        wait_apart(pool, (hid_silu, FC * f + c + 1), (down_done, FC * f + c - HR + 1))
                        nc.gpsimd.tensor_scalar(h_hi[:, c % HR, :], hidden[:, c % SR, :], 1.0, 1.0,
                                                ALU.mult, ALU.mult).then_inc(hid_hi_pool, 1)
                    d = c - LAG - 1
                    if d >= 2 * FJ - 1 and d % FJ == FJ - 1:
                        add_output(d // FJ)
                    if beside and c < FC + LAG:
                        beside(c)

            def attention(a, m, beside):
                def add_products(w):
                    hp, j = divmod(w, 4)
                    if j == 1:
                        pool.wait_ge(rot_mul, UNITS * a + w + 1)
                        if hp >= 2:
                            pool.wait_ge(s_made, PAIRS * a + NT * (hp - 1))
                        nc.gpsimd.tensor_tensor(q_rot[hp % 2], hidden[:, 0, :], hidden[:, 1, :],
                                                ALU.add).then_inc(q_ready, 1)
                    if j == 3:
                        pool.wait_ge(rot_mul, UNITS * a + w + 1)
                        if hp >= 2:
                            pool.wait_ge(s_made, PAIRS * a + NT * (hp - 1))
                        nc.gpsimd.tensor_tensor(hidden[:, 2, :], hidden[:, 2, :], hidden[:, 3, :],
                                                ALU.add).then_inc(k_added, 1)
                        wait_apart(pool, (k_added, HP * a + hp + 1))
                        for h in range(2):
                            nc.gpsimd.tensor_scalar(k_diag[hp % 2][:, :, OWN[h]:OWN[h] + P],
                                                    hidden[:, 2, :].rearrange("p (t n) -> p t n", t=NT),
                                                    head_rows[:, h:h + 1], 1.0, ALU.mult, ALU.mult)
                        nc.gpsimd.tensor_scalar(k_diag[hp % 2][:, :, PERSISTENT],
                                                pmk_sb[:, hp:hp + 1, :].broadcast_to([P, NT, 2 * PM]),
                                                1.0, 1.0, ALU.mult, ALU.mult).then_inc(k_ready, 1)

                for w in range(LEAD):
                    add_products(w)
                for s in range(SLOTS):
                    if s + LEAD < UNITS:
                        add_products(s + LEAD)
                    beside(s)

            def prep(slot, role, n, r, m, src, loads=None):
                for step in steps_of(slot, PREP):
                    if step == 1:
                        count = [0]

                        def link(ins):
                            count[0] += 1
                            ins.then_inc(rstd_self, 1)
                            wait_apart(pool, (rstd_self, 6 * n + count[0]))
                        wait_apart(pool, (stats_ready, n + 1))
                        link(nc.gpsimd.tensor_scalar(rstd[:, 0, :], mean_var[:, :, 1], 1.0, LN_EPS, ALU.mult, ALU.add))
                        ln = nc.gpsimd.tensor_tensor(rstd[:, 1, :], rstd[:, 0, :], minus_half[:], ALU.pow)
                        link(ln)
                        link(nc.gpsimd.tensor_tensor(rstd[:, 2, :], rstd[:, 1, :], rstd[:, 1, :], ALU.mult))
                        link(nc.gpsimd.tensor_tensor(rstd[:, 2, :], rstd[:, 2, :], mean_var[:, :, 1], ALU.mult))
                        link(nc.gpsimd.tensor_scalar(rstd[:, 2, :], rstd[:, 2, :], 1.0, RMS_EPS, ALU.mult, ALU.add))
                        link(nc.gpsimd.tensor_tensor(rstd[:, 3, :], rstd[:, 2, :], minus_half[:], ALU.pow))
                        nc.gpsimd.tensor_tensor(rstd[:, 3, :], rstd[:, 3, :], rstd[:, 1, :], ALU.mult).then_inc(rstd_ready, 1)

            def finish(slot, role, m, count, g):
                pass

            program(nc.gpsimd, ffn, attention, prep, finish, start)


def stage(values, slot):
    return values[:, slot // 2, slot % 2 * N:(slot % 2 + 1) * N]


def x_hat_stage(values):
    return values[0:96, NT - 1, :].rearrange("p (h d) -> p h d", h=HP)


def blocks_before(experts):
    rest = BLOCKS - Q_AT
    experts = min(experts, FE)
    return 2 * experts + (rest * (experts - 1) + FE - 2) // (FE - 1)


def split_order():
    order = []
    for e in range(FE):
        order += [2 * e, 2 * e + 1]
        while len(order) < blocks_before(e + 1):
            order.append(Q_AT + len(order) - 2 * (e + 1))
    return order


def kernel(L0_attn_seq, L0_attn_g_norm, L0_attn_W_qkv, L0_attn_W_out, L0_attn_pm,
           L0_ffn_shared_w1, L0_ffn_shared_w2, L0_ffn_experts_w1, L0_ffn_experts_w2, L0_ffn_gate_w):
    import numpy as np
    import concourse.bacc as bacc
    from concourse import mybir as mb
    from concourse.bass_utils import run_bass_kernel_spmd

    seq, wqkv, wout, pm = (np.asarray(a) for a in (L0_attn_seq, L0_attn_W_qkv, L0_attn_W_out, L0_attn_pm))
    b, s, d = seq.shape
    groups = b * s // N
    x = seq.reshape(groups, NT, P, d).transpose(0, 2, 1, 3)
    shape = x.shape
    x = np.concatenate([x, x[:1]])

    half = np.arange(DH // 2)
    channel = np.concatenate([2 * half, 2 * half, 2 * half + 1, 2 * half + 1])
    head = np.repeat([0, 1, 0, 1], DH // 2)
    cols = (np.arange(HP)[:, None] * 2 + head) * DH + channel
    cols = np.concatenate([cols, cols[:, :DH]], axis=1).reshape(-1)
    inner = HEADS * DH
    w1 = np.concatenate([np.asarray(L0_ffn_shared_w1)[None], np.asarray(L0_ffn_experts_w1)])
    w2 = np.concatenate([np.asarray(L0_ffn_shared_w2)[None], np.asarray(L0_ffn_experts_w2)])
    w1 = w1.transpose(2, 0, 1)
    w2 = w2.reshape(FE, d, FJ, P).transpose(3, 0, 2, 1).reshape(P, FE, FJ * d)
    experts = np.stack([w1, w2], axis=2).reshape(P, -1)
    weights = np.concatenate([experts, wqkv[:, cols], wqkv[:, inner + cols], wqkv[:, 2 * inner:],
                              wout.reshape(HP, P, d).transpose(1, 0, 2).reshape(P, -1)], axis=1)

    pm_k = np.zeros((P, HP, 2, PM), pm.dtype)
    pm_v = np.zeros((3, 2, PM, HP, 2, DH), pm.dtype)
    for h in range(2):
        pm_k[head == h, :, h, :] = pm[0, h::2][:, :, channel[head == h]].transpose(2, 0, 1)
        pm_v[:, h, :, :, h, :] = pm[1, h::2].transpose(1, 0, 2)
    pm_k, pm_v = pm_k.reshape(P, HP, 2 * PM), pm_v.reshape(96, HP, P)

    freq = np.float32(1) / np.float32(10000.0) ** (np.arange(0, DH, 2, dtype=np.float32) / np.float32(DH))
    angle = (np.arange(s, dtype=np.float32)[:, None] * freq).T.astype(np.float32)
    angle = angle[channel // 2]
    cos, sin = np.cos(angle), np.where(channel[:, None] % 2, np.sin(angle), -np.sin(angle))
    rotary = np.stack([cos * DH ** -0.5, sin * DH ** -0.5, cos, sin], axis=1).astype(np.float32)

    ins = {"x": x, "weights": weights, "gate_w": np.asarray(L0_ffn_gate_w).T, "g_norm": np.asarray(L0_attn_g_norm)[:, None],
           "pm_k": pm_k, "pm_v": pm_v, "rotary": rotary}
    nc = bacc.Bacc("TRN2", target_bir_lowering=False, num_devices=1)
    arrays, args = {}, []
    for name, a in ins.items():
        arrays[name] = np.ascontiguousarray(a)
        args.append(nc.dram_tensor(name, a.shape, mb.dt.from_np(a.dtype), kind="ExternalInput").ap())
    args.append(nc.dram_tensor("out", shape, mb.dt.float32, kind="ExternalOutput").ap())
    macaron(nc, *args)
    r = run_bass_kernel_spmd(nc, [arrays], core_ids=[0])
    out = np.asarray(r.results[0]["out"])
    return out.transpose(0, 2, 1, 3).reshape(b, s, d)
```

```python
from contextlib import ExitStack

import concourse.bass as bass
from concourse import mybir

F32 = mybir.dt.float32
F32R = mybir.dt.float32r
BF16 = mybir.dt.bfloat16
ALU = mybir.AluOpType
ACT = mybir.ActivationFunctionType
AX_X = mybir.AxisListType.X

P = 128
N = 512
NT = N // P
HEADS, DH, SEG, PM = 16, 64, 64, 16
HP = HEADS // 2
PAIRS = HP * NT
KEYS = P + PM
OWN = (0, P + 2 * PM)
PERSISTENT = slice(P, P + 2 * PM)
EXPERTS = 8
FE = 1 + EXPERTS
FJ = 4
FC = FE * FJ
LN_EPS = 1e-5
RMS_EPS = 2.0 ** -23
MASKED = -1e30

QK_COLS = 3 * DH
Q_AT = 2 * FE
K_AT = Q_AT + HP * QK_COLS // N
V_AT = K_AT + HP * QK_COLS // N
OUT_AT = V_AT + 2
BLOCKS = OUT_AT + 2
STAGES = 8

LAG = 3
SR = 4
HR = 3
PR = 3
LEAD = 6
UNITS = 4 * HP
TAIL = LAG + 1
HEAD = 4
T_LAG, AV_LAG = 2, 3
O_LAG = NT - 1 + AV_LAG
W_LAG = O_LAG + 3
SLOTS = NT * (HP - 1) + W_LAG + 1

PREP = {"stats": 0, "variance": 1, "rstd": 1, "rms": 2, "rms_rstd": 3, "x_hat": 5, "x_hat_rest": 6,
        "transpose": 10, "split": 10, "logits": 14, "copy": 14, "compare": 15, "ties": 16, "rank": 17,
        "chosen": 17, "centre": 18, "tanh": 19, "gates": 19, "gates_t": 23, "gates_split": 23}
FINISH = {"transpose": 0, "add": 0}


def macaron(nc, x_in, weights, gate_w, g_norm, pm_k, pm_v, rotary, x_out):
    groups = x_in.shape[0] - 1
    ctx = ExitStack()
    with ctx:
        def sb(name, shape, dt=F32):
            return ctx.enter_context(nc.sbuf_tensor(name, shape, dt))

        def sem(name):
            return ctx.enter_context(nc.semaphore(name))

        w_hi = sb("w_hi", [P, BLOCKS * N], F32R)
        w_lo = sb("w_lo", [P, BLOCKS * N], F32R)
        values = sb("values", [P, NT, HEADS * DH])
        k_diag = [sb(f"k_diag{i}", [P, NT, 2 * KEYS]) for i in range(2)]
        hidden = sb("hidden", [P, SR, N])
        h_hi = sb("h_hi", [P, HR, N], F32R)
        h_lo = sb("h_lo", [P, HR, N], F32R)
        scratch = sb("scratch", [P, 4 * N])
        gate_cols = [scratch[:, i * N:(i + 1) * N] for i in range(2)]
        gated = [scratch[:, (2 + i) * N:(3 + i) * N] for i in range(2)]
        q_rot = [scratch[:, i * N:(i + 1) * N] for i in range(2)]
        probs = [scratch[:, 2 * N + i * 2 * KEYS:2 * N + (i + 1) * 2 * KEYS]
                 for i in range(PR)]
        probs_t = sb("probs_t", [P, 2, 2 * P])
        pm_t = [x[0:6 * PM, 2, :] for x in (h_hi, h_lo)]
        pm_parts = sb("pm_parts", [P, 2, 6 * PM], F32R)
        norm_hi = [sb(f"norm_hi{i}", [P, N], F32R) for i in range(3)]
        norm_lo = [sb(f"norm_lo{i}", [P, N], F32R) for i in range(3)]
        gates_t = [sb(f"gates_t{i}", [DH, N], F32R) for i in range(2)]
        x1 = sb("x1", [P, NT, P])
        x2 = sb("x2", [P, NT, P])
        x3 = sb("x3", [P, NT, P])
        x_hat = sb("x_hat", [P, NT, P])
        acc = sb("acc", [P, N])
        tables = sb("tables", [P, 4, N // 2])
        ident = sb("ident", [P, P])
        ident_bf = sb("ident_bf", [P, P], BF16)
        mask_bf = sb("mask_bf", [P, 2 * KEYS], BF16)
        gate_raw = sb("gate_raw", [P, EXPERTS])
        gate_hi = sb("gate_hi", [P, EXPERTS], F32R)
        gate_lo = sb("gate_lo", [P, EXPERTS], F32R)
        pick_raw = sb("pick_raw", [DH, EXPERTS])
        pick = sb("pick", [DH, EXPERTS], F32R)
        below = sb("below", [P, EXPERTS, EXPERTS])
        above = sb("above", [P, EXPERTS, EXPERTS])
        head_rows = sb("head_rows", [P, 2])
        g_col = sb("g_col", [P, 1])
        pmk_sb = sb("pmk_sb", [P, HP, 2 * PM])
        pmv_sb = sb("pmv_sb", [96, HP, P], F32R)
        stats = sb("stats", [P, NT, 6])
        mean_vars = [sb(f"mean_var{i}", [P, NT, 2]) for i in range(2)]
        rstd = sb("rstd", [P, 4, NT])
        minus_half = sb("minus_half", [P, NT])
        logits = sb("logits", [P, NT, EXPERTS])
        top8 = sb("top8", [P, NT, EXPERTS])
        cmp_ge, cmp_gt = (x_hat[:, i:i + NT // 2, :].rearrange("p a (b e j) -> p (a b) e j", e=EXPERTS, j=EXPERTS)
                          for i in (0, NT // 2))
        rank = sb("rank", [P, NT, EXPERTS])
        top_sum = sb("top_sum", [P, NT, 1])
        centred = sb("centred", [P, NT, EXPERTS])
        tanhs = sb("tanhs", [P, NT, EXPERTS])
        gates = sb("gates", [P, NT, EXPERTS])
        neg_max = sb("neg_max", [P, 4, 2])
        row_sum = sb("row_sum", [P, 4, 2])
        row_inv = sb("row_inv", [P, 4, 2])
        warm = sb("warm", [P, 1])

        bank = [ctx.enter_context(nc.psum_tensor(f"bank{i}", [P, N], F32)) for i in range(8)]
        side = bank[7]

        ld_x, ld_small, ld_pmv, st_out = sem("ld_x"), sem("ld_small"), sem("ld_pmv"), sem("st_out")
        ld_w = [sem(f"ld_w{i}") for i in range(STAGES)]
        split_hi, split_lo = sem("split_hi"), sem("split_lo")
        consts_pool, consts_act, consts_dve, pool_self = sem("consts_pool"), sem("consts_act"), sem("consts_dve"), sem("pool_self")
        hid_made, hid_silu, hid_hi_act, hid_hi_pool, hid_lo = (
            sem("hid_made"), sem("hid_silu"), sem("hid_hi_act"), sem("hid_hi_pool"), sem("hid_lo"))
        down_done, y_used, gcols_made, gcols_copied, acc_added = (
            sem("down_done"), sem("y_used"), sem("gcols_made"), sem("gcols_copied"), sem("acc_added"))
        side_made, side_used = sem("side_made"), sem("side_used")
        passed = sem("passed")
        stats_ready, rstd_ready, xhat_ready, norm_hi_ready = (
            sem("stats_ready"), sem("rstd_ready"), sem("xhat_ready"), sem("norm_hi_ready"))
        prep_self, norm_self, centred_ready, tanh_ready, gates_ready, gates_hi_ready = (
            sem("prep_self"), sem("norm_self"), sem("centred_ready"), sem("tanh_ready"), sem("gates_ready"), sem("gates_hi_ready"))
        v_made, v_copied, proj_made, rot_mul, q_ready, k_ready, k_added, rstd_self = (
            sem("v_made"), sem("v_copied"), sem("proj_made"), sem("rot_mul"), sem("q_ready"), sem("k_ready"),
            sem("k_added"), sem("rstd_self"))
        norm_done_act, rms_self, parts_hi, o_raw = sem("norm_done_act"), sem("rms_self"), sem("parts_hi"), sem("o_raw")
        s_made, max_ready, exp_done, inv_ready, p_ready = (
            sem("s_made"), sem("max_ready"), sem("exp_done"), sem("inv_ready"), sem("p_ready"))
        t_made, t_copied, norm_done, av_done = (
            sem("t_made"), sem("t_copied"), sem("norm_done"), sem("av_done"))
        o_hi, o_lo, wout_done, yatt_copied = sem("o_hi"), sem("o_lo"), sem("wout_done"), sem("yatt_copied")

        def w1(part, e, j):
            return part[:, 2 * e * N + j * P:2 * e * N + (j + 1) * P]

        def w2(part, e, j):
            return part[:, (2 * e + 1) * N + j * P:(2 * e + 1) * N + (j + 1) * P]

        def y_bank(e, f, role):
            odd = f % 2 if isinstance(f, int) else 1 - role // 2
            return bank[4 + (e + odd) % 2][:]

        def wait(eng, s, value):
            if not isinstance(value, int) or value > 0:
                eng.wait_ge(s, value)

        def wait_apart(eng, *waits):
            for s, v in waits:
                wait(eng, s, v)
            eng.sem_inc(passed, 1)

        def program(eng, ffn_slot, ffn, attention, prep, finish, start):
            start()
            prep(None, role=0, n=0, r=0, m=0, src=x1, loads=1)
            ffn(None, f=0, role=0, m=0, before=None, splits=True)
            for c in range(FC, FC + TAIL):
                ffn_slot(c, f=0, role=0)
            finish(None, role=0, m=3, count=0, g=0)
            prep(None, role=1, n=1, r=0, m=4, src=x2)

            def beside_first_attention(slot):
                prep(slot - 3, role=0, n=2, r=1, m=5, src=x1, loads=2)
            attention(a=0, m=4, beside=beside_first_attention, before=None, then=dict(f=1, role=0, m=5))

            with eng.Fori(0, groups - 1) as g:
                def beside_first_ffn(slot):
                    finish(slot - 4, role=1, m=10 * g + 8, count=g, g=g)
                    prep(slot - 7, role=2, n=3 * g + 3, r=2 * g + 2, m=10 * g + 9, src=x3)
                ffn(beside_first_ffn, f=2 * g + 1, role=0, m=10 * g + 5, before="attention", attentions=g + 1)

                def beside_second_ffn(slot):
                    finish(slot - 5, role=0, m=10 * g + 12, count=2 * g + 1, g=g)
                    prep(slot - 7, role=1, n=3 * g + 4, r=g + 1, m=10 * g + 13, src=x2)
                    prep(slot - 12, role=0, n=3 * g + 5, r=2 * g + 3, m=10 * g + 14, src=x1, loads=g + 3)
                ffn(beside_second_ffn, f=2 * g + 2, role=2, m=10 * g + 9, before=dict(f=2 * g + 1, role=0))

                def beside_attention(slot):
                    finish(slot - 4, role=2, m=10 * g + 17, count=2 * g + 2, g=g)
                attention(a=g + 1, m=10 * g + 13, beside=beside_attention, before=dict(f=2 * g + 2, role=2),
                          then=dict(f=2 * g + 3, role=0, m=10 * g + 14))

            g = groups - 1
            finish(None, role=1, m=10 * g + 8, count=g, g=g)
            prep(None, role=2, n=3 * g + 3, r=2 * g + 2, m=10 * g + 9, src=x3)
            ffn(None, f=2 * g + 1, role=2, m=10 * g + 9, before=None, unused=HEAD)
            for c in range(FC, FC + TAIL):
                ffn_slot(c, f=2 * g + 1, role=2, unused=HEAD)
            finish(None, role=2, m=10 * g + 12, count=2 * g + 1, g=g)

        def steps_of(slot, schedule):
            return [step for step, at in schedule.items() if slot is None or at == slot]

        block = ctx.enter_context(nc.Block())

        @block.sync
        def _(sp):
            sp.sem_inc(st_out, 16)
            sp.dma_start(x1[:], x_in[0]).then_inc(ld_x, 16)
            for dst, src in ((gate_raw[:], gate_w), (g_col[:], g_norm), (pmk_sb[:], pm_k), (tables[:], rotary)):
                sp.dma_start(dst, src).then_inc(ld_small, 16)
            sp.dma_start(x_hat_stage(values), pm_v).then_inc(ld_pmv, 16)
            for b, blk in enumerate(split_order()):
                slot = b % (STAGES - 2)
                if b >= STAGES - 2:
                    sp.wait_ge(split_lo, b - (STAGES - 2) + 1)
                sp.dma_start(stage(values, slot), weights[:, blk * N:(blk + 1) * N]).then_inc(ld_w[slot], 16)
            sp.wait_ge(side_used, 4)
            sp.dma_start(x1[:], x_in[1]).then_inc(ld_x, 16)
            with sp.Fori(0, groups - 1) as g:
                wait_apart(sp, (side_used, 10 * g + 13))
                sp.dma_start(x1[:], x_in[2:][g]).then_inc(ld_x, 16)
                wait_apart(sp, (side_used, 10 * g + 18))
                sp.dma_start(x_out[g], x3[:]).then_inc(st_out, 16)
            sp.wait_ge(side_used, 10 * (groups - 1) + 13)
            sp.dma_start(x_out[groups - 1], x3[:]).then_inc(st_out, 16)
            sp.wait_ge(st_out, 16 * (groups + 1))
            sp.wait_ge(ld_x, 16 * (groups + 1))

        @block.tensor
        def _(pe):
            def split3(out, lhs_hi, lhs_lo, rhs_hi, rhs_lo, start, stop):
                nc.tensor.matmul(out, lhs_hi, rhs_hi, start=start, stop=False)
                nc.tensor.matmul(out, lhs_hi, rhs_lo, start=False, stop=False)
                return nc.tensor.matmul(out, lhs_lo, rhs_hi, start=False, stop=stop)

            def start():
                pe.wait_ge(consts_pool, 1)
                pe.wait_ge(consts_dve, 1)

            def first_product(c, f, role, m, unused=0):
                if c == 0:
                    pe.wait_ge(side_used, m + 1)
                e, j = divmod(c, FJ)
                wait(pe, hid_silu, FC * f + unused + c - 3)
                split3(bank[c % 4][:], w1(w_hi, e, j), w1(w_lo, e, j), norm_hi[role][:],
                       norm_lo[role][:], True, True).then_inc(hid_made, 1)

            def spread_gates(e, f, role, m, attentions):
                if e == 1:
                    pe.wait_ge(side_used, m + 3)
                    if attentions is not None:
                        pe.wait_ge(yatt_copied, attentions)
                wait(pe, gcols_copied, EXPERTS * f + e - 1)
                nc.tensor.matmul(bank[6][:], pick[:, e - 1:e].broadcast_to([DH, P]),
                                 gates_t[role // 2][:], start=True, stop=True).then_inc(gcols_made, 1)

            def ffn_slot(c, f, role, m=None, begun=0, attentions=None, unused=0, splits=False):
                if splits and c < FC and c % FJ == 0:
                    pe.wait_ge(split_lo, blocks_before(c // FJ + 1))
                if FJ <= c < FC and c % FJ == 0:
                    spread_gates(c // FJ, f, role, m, attentions)
                if begun <= c < FC:
                    first_product(c, f, role, m, unused)
                if LAG <= c < FC + LAG:
                    d = c - LAG
                    e, j = divmod(d, FJ)
                    if j == 0:
                        wait(pe, y_used, FE * f + e - 1)
                    pe.wait_ge(hid_lo, FC * f + d + 1)
                    split3(y_bank(e, f, role), w2(w_hi, e, j), w2(w_lo, e, j), h_hi[:, d % HR, :],
                           h_lo[:, d % HR, :], j == 0, j == FJ - 1).then_inc(down_done, 1)

            def ffn(beside, f, role, m, before, attentions=None, unused=0, splits=False):
                for c in range(FC):
                    ffn_slot(c, f, role, m, HEAD if before == "attention" else 0, attentions, unused, splits)
                    if isinstance(before, dict) and c < TAIL:
                        ffn_slot(FC + c, **before)
                    if beside:
                        beside(c)

            def attention(a, m, beside, before, then):
                xh, xl = norm_hi[1], norm_lo[1]
                pe.wait_ge(side_used, m + 1)
                if isinstance(a, int):
                    pe.wait_ge(split_lo, BLOCKS)
                def values_unit(v):
                    t, half = divmod(v, 2)
                    if v >= 2:
                        pe.wait_ge(v_copied, 2 * NT * a + v - 1)
                    cols = slice((V_AT + half) * N, (V_AT + half + 1) * N)
                    rows = slice(t * P, (t + 1) * P)
                    split3(bank[2 + v % 2][:], xh[:, rows], xl[:, rows], w_hi[:, cols], w_lo[:, cols],
                           True, True).then_inc(v_made, 1)

                def project(w):
                    hp, j = divmod(w, 4)
                    if w >= 2:
                        pe.wait_ge(rot_mul, UNITS * a + w - 1)
                    at = (Q_AT, K_AT)[j // 2] * N + hp * QK_COLS + j % 2 * DH
                    parts = [x[:, at:at + P] for x in (w_hi, w_lo)]
                    split3(bank[w % 2][:], *parts, xh[:], xl[:], True, True).then_inc(proj_made, 1)

                def scores(s):
                    hp, p = divmod(s, NT)
                    if p == 0:
                        pe.wait_ge(q_ready, HP * a + hp + 1)
                        pe.wait_ge(k_ready, HP * a + hp + 1)
                    if s >= 2:
                        pe.wait_ge(exp_done, 2 * (PAIRS * a + s - 1))
                    else:
                        pe.wait_ge(v_copied, 2 * NT * a + 2 * NT)
                    out = bank[2 + s % 2][:, 0:2 * KEYS]
                    nc.tensor.matmul(out, ident_bf[:], mask_bf[:], start=True, stop=False)
                    nc.tensor.matmul(out, q_rot[hp % 2][:, p * P:(p + 1) * P],
                                     k_diag[hp % 2][:, p], start=False, stop=True).then_inc(s_made, 1)

                def transpose(s):
                    pe.wait_ge(p_ready, PAIRS * a + s + 1)
                    if s >= 1:
                        pe.wait_ge(t_copied, PAIRS * a + s)
                    for h in range(2):
                        nc.tensor.transpose(bank[4][:, h * P:(h + 1) * P], probs[s % PR][:, OWN[h]:OWN[h] + P], ident[:])
                    nc.tensor.transpose(bank[4][0:6 * PM, 2 * P:3 * P], pm_parts[:, s % 2, :].bitcast(F32),
                                        ident[:]).then_inc(t_made, 1)

                def weigh_values(s):
                    hp, p = divmod(s, NT)
                    pe.wait_ge(t_copied, PAIRS * a + s + 1)
                    if p == 0 and hp >= 1:
                        pe.wait_ge(o_raw, HP * a + hp)
                    for h in range(2):
                        head = slice((2 * hp + h) * DH, (2 * hp + h + 1) * DH)
                        last = nc.tensor.matmul(bank[5][h * DH:(h + 1) * DH, p * P:(p + 1) * P],
                                                values[:, p, head], probs_t[:, s % 2, h * P:(h + 1) * P],
                                                start=p == 0, stop=False, skip_group_check=True)
                    if p == NT - 1:
                        last = nc.tensor.matmul(bank[5][:], pmv_sb[:, hp, :], pm_t[hp % 2][:],
                                                start=False, stop=True, skip_group_check=True)
                    last.then_inc(av_done, 1)

                def times_w_out(hp):
                    pe.wait_ge(o_lo, HP * a + hp + 1)
                    cols = slice(OUT_AT * N + hp * P, OUT_AT * N + (hp + 1) * P)
                    split3(bank[6][:], w_hi[:, cols], w_lo[:, cols], h_hi[:, hp % 2, :], h_lo[:, hp % 2, :],
                           hp == 0, hp == HP - 1).then_inc(wout_done, 1)

                if before:
                    pe.wait_ge(hid_silu, FC * (before["f"] + 1))
                for v in range(2 * NT):
                    if v < LEAD:
                        project(v)
                    values_unit(v)
                    if before and v < TAIL:
                        ffn_slot(FC + v, **before)
                for s in range(SLOTS):
                    if s < PAIRS:
                        scores(s)
                    if s + LEAD < UNITS:
                        project(s + LEAD)
                    if 0 <= s - PAIRS < HEAD:
                        first_product(s - PAIRS, **then)
                    if 0 <= s - T_LAG < PAIRS:
                        transpose(s - T_LAG)
                    if 0 <= s - AV_LAG < PAIRS:
                        weigh_values(s - AV_LAG)
                    if s >= W_LAG and (s - W_LAG) % NT == 0:
                        times_w_out((s - W_LAG) // NT)
                    beside(s)

            def prep(slot, role, n, r, m, src, loads=None):
                for step in steps_of(slot, PREP):
                    if step == "transpose":
                        pe.wait_ge(xhat_ready, n + 1)
                        wait(pe, side_used, m)
                        for t in range(NT):
                            last = nc.tensor.transpose(side[:, t * P:(t + 1) * P], x_hat[:, t, :], ident[:])
                        last.then_inc(side_made, 1)
                    if step == "logits" and role != 1:
                        pe.wait_ge(side_used, m + 1)
                        for t in range(NT):
                            rows = slice(t * P, (t + 1) * P)
                            last = split3(side[:, t * EXPERTS:(t + 1) * EXPERTS], norm_hi[role][:, rows],
                                          norm_lo[role][:, rows], gate_hi[:], gate_lo[:], True, True)
                        last.then_inc(side_made, 1)
                    if step == "gates_t" and role != 1:
                        pe.wait_ge(gates_ready, r + 1)
                        pe.wait_ge(side_used, m + 2)
                        for t in range(NT):
                            last = nc.tensor.transpose(side[0:EXPERTS, t * P:(t + 1) * P], gates[:, t, :], ident[:])
                        last.then_inc(side_made, 1)

            def finish(slot, role, m, count, g):
                for step in steps_of(slot, FINISH):
                    if step == "transpose":
                        if role == 1:
                            pe.wait_ge(yatt_copied, count + 1)
                        else:
                            pe.wait_ge(acc_added, EXPERTS * (count + 1))
                        pe.wait_ge(side_used, m)
                        for t in range(NT):
                            last = nc.tensor.transpose(side[:, t * P:(t + 1) * P], acc[:, t * P:(t + 1) * P], ident[:])
                        last.then_inc(side_made, 1)

            program(nc.tensor, ffn_slot, ffn, attention, prep, finish, start)

        @block.scalar
        def _(act):
            def split_block(b, blk):
                slot = b % (STAGES - 2)
                act.wait_ge(ld_w[slot], 16 * (b // (STAGES - 2) + 1))
                nc.scalar.activation(w_hi[:, blk * N:(blk + 1) * N], stage(values, slot), ACT.Copy).then_inc(split_hi, 1)

            order = split_order()

            def start():
                act.wait_ge(ld_small, 16 * 4)
                nc.scalar.activation(gate_hi[:], gate_raw[:], ACT.Copy)
                act.wait_ge(consts_pool, 2)
                nc.scalar.activation(pick[:], pick_raw[:], ACT.Copy)
                act.wait_ge(ld_pmv, 16)
                nc.scalar.activation(pmv_sb[:], x_hat_stage(values), ACT.Copy).then_inc(consts_act, 1)
                for b in range(blocks_before(1)):
                    split_block(b, order[b])

            def silu(c, f, role, unused=0):
                act.wait_ge(hid_made, FC * f + unused + c + 1)
                wait(act, hid_lo, FC * f + c - SR + 1)
                nc.scalar.activation(hidden[:, c % SR, :], bank[c % 4][:], ACT.Silu).then_inc(hid_silu, 1)

            def ffn_slot(c, f, role, begun=0, unused=0):
                if begun <= c < FC:
                    silu(c, f, role, unused)
                d = c - 1
                if 0 <= d < FC and d % 2 == 1:
                    act.wait_ge(hid_silu, FC * f + unused + d + 1)
                    wait(act, down_done, FC * f + d - HR + 1)
                    nc.scalar.activation(h_hi[:, d % HR, :], hidden[:, d % SR, :], ACT.Copy).then_inc(hid_hi_act, 1)
                if FJ <= c < FC and c % FJ == 0:
                    e = c // FJ
                    act.wait_ge(gcols_made, EXPERTS * f + e)
                    wait(act, y_used, FE * f + e - 1)
                    nc.scalar.activation(gate_cols[e % 2], bank[6][:], ACT.Copy).then_inc(gcols_copied, 1)

            def ffn(beside, f, role, m, before, attentions=None, unused=0, splits=False):
                for c in range(FC):
                    if splits and c % FJ == 0:
                        for b in range(blocks_before(c // FJ + 1), blocks_before(c // FJ + 2)):
                            split_block(b, order[b])
                    ffn_slot(c, f, role, HEAD if before == "attention" else 0, unused)
                    if isinstance(before, dict) and c < TAIL:
                        ffn_slot(FC + c, **before)
                    if beside:
                        beside(c)
                if role == 2 or splits:
                    nc.scalar.activation(warm[:], minus_half[:, 0:1], ACT.Exp)

            def attention(a, m, beside, before, then):
                for v in range(2 * NT):
                    if before and v < TAIL:
                        ffn_slot(FC + v, **before)
                    t, half = divmod(v, 2)
                    act.wait_ge(v_made, 2 * NT * a + v + 1)
                    nc.scalar.activation(values[:, t, half * N:(half + 1) * N], bank[2 + v % 2][:],
                                         ACT.Copy).then_inc(v_copied, 1)

                def exps(s):
                    act.wait_ge(max_ready, PAIRS * a + s + 1)
                    if s >= PR:
                        act.wait_ge(t_made, PAIRS * a + s - PR + 1)
                    for h in range(2):
                        nc.scalar.activation(probs[s % PR][:, h * KEYS:(h + 1) * KEYS], bank[2 + s % 2][:, h * KEYS:(h + 1) * KEYS],
                                             ACT.Exp, bias=neg_max[:, s % 4, h:h + 1],
                                             accum_out=row_sum[:, s % 4, h:h + 1]).then_inc(exp_done, 1)

                def copy_transposed(s):
                    hp, p = divmod(s, NT)
                    act.wait_ge(t_made, PAIRS * a + s + 1)
                    if s >= 2:
                        act.wait_ge(av_done, PAIRS * a + s - 1)
                    nc.scalar.activation(pm_t[hp % 2][:, p * P:(p + 1) * P], bank[4][0:6 * PM, 2 * P:3 * P], ACT.Copy)
                    nc.scalar.activation(probs_t[:, s % 2, :], bank[4][:, 0:2 * P], ACT.Copy).then_inc(t_copied, 1)

                def copy_output(hp):
                    act.wait_ge(av_done, PAIRS * a + NT * (hp + 1))
                    if hp >= 1:
                        act.wait_ge(o_lo, HP * a + hp)
                    nc.scalar.activation(acc[:], bank[5][:], ACT.Copy).then_inc(o_raw, 1)

                def normalise_second(s):
                    act.wait_ge(inv_ready, PAIRS * a + s + 1)
                    part = probs[s % PR][:, KEYS:2 * KEYS]
                    nc.scalar.activation(part, part, ACT.Copy, scale=row_inv[:, s % 4, 1:2]).then_inc(norm_done_act, 1)

                for s in range(SLOTS):
                    if 0 <= s - 1 < PAIRS:
                        normalise_second(s - 1)
                    if s < PAIRS:
                        exps(s)
                    if 0 <= s - T_LAG < PAIRS:
                        copy_transposed(s - T_LAG)
                    if s >= O_LAG and (s - O_LAG) % NT == 0 and (s - O_LAG) // NT < HP:
                        copy_output((s - O_LAG) // NT)
                    if 0 <= s - PAIRS < HEAD:
                        if s == PAIRS:
                            act.wait_ge(k_ready, HP * (a + 1))
                        silu(s - PAIRS, then["f"], then["role"])
                    beside(s)
                act.wait_ge(wout_done, HP * (a + 1))
                nc.scalar.activation(acc[:], bank[6][:], ACT.Copy).then_inc(yatt_copied, 1)

            def prep(slot, role, n, r, m, src, loads=None):
                for step in steps_of(slot, PREP):
                    if step == "split":
                        act.wait_ge(side_made, m + 1)
                        scale = g_col[:, 0:1] if role == 1 else 1.0
                        nc.scalar.activation(norm_hi[role][:], side[:], ACT.Copy, scale=scale).then_inc(norm_hi_ready, 1)
                    if step == "tanh" and role != 1:
                        act.wait_ge(centred_ready, r + 1)
                        nc.scalar.activation(tanhs[:], centred[:], ACT.Tanh).then_inc(tanh_ready, 1)
                    if step == "gates_split" and role != 1:
                        act.wait_ge(side_made, m + 3)
                        nc.scalar.activation(gates_t[role // 2][0:EXPERTS, :], side[0:EXPERTS, :],
                                             ACT.Copy).then_inc(gates_hi_ready, 1)

            def finish(slot, role, m, count, g):
                pass

            program(nc.scalar, ffn_slot, ffn, attention, prep, finish, start)

        @block.vector
        def _(dve):
            order = split_order()

            def split_block(b, blk):
                slot = b % (STAGES - 2)
                dve.wait_ge(split_hi, b + 1)
                cols = slice(blk * N, (blk + 1) * N)
                nc.vector.tensor_tensor(w_lo[:, cols], stage(values, slot), w_hi[:, cols].bitcast(F32),
                                        ALU.subtract).then_inc(split_lo, 1)

            def start():
                dve.wait_ge(consts_act, 1)
                nc.vector.tensor_tensor(gate_lo[:], gate_raw[:], gate_hi[:].bitcast(F32), ALU.subtract)
                low = slice(64, 96)
                nc.vector.tensor_tensor(pmv_sb[low], x_hat_stage(values)[low], pmv_sb[low].bitcast(F32),
                                        ALU.subtract).then_inc(consts_dve, 1)
                dve.wait_ge(consts_pool, 3)

            def use_output(e, f, role):
                dve.wait_ge(down_done, FC * f + FJ * (e + 1))
                y = y_bank(e, f, role)
                if e == 0:
                    nc.vector.tensor_scalar(acc[:], y, 0.5, None, ALU.mult).then_inc(y_used, 1)
                else:
                    dve.wait_ge(gcols_copied, EXPERTS * f + e)
                    if e >= 3:
                        dve.wait_ge(acc_added, EXPERTS * f + e - 2)
                    nc.vector.tensor_tensor(gated[e % 2], y, gate_cols[e % 2], ALU.mult).then_inc(y_used, 1)

            def ffn_slot(c, f, role, unused=0):
                if c < FC:
                    dve.wait_ge(hid_silu, FC * f + unused + c + 1)
                    if c % 2:
                        dve.wait_ge(hid_hi_act, FC // 2 * f + c // 2 + 1)
                    else:
                        dve.wait_ge(hid_hi_pool, FC // 2 * f + c // 2 + 1)
                    wait(dve, down_done, FC * f + c - HR + 1)
                    nc.vector.tensor_tensor(h_lo[:, c % HR, :], hidden[:, c % SR, :],
                                            h_hi[:, c % HR, :].bitcast(F32), ALU.subtract).then_inc(hid_lo, 1)
                if FJ - 1 + LAG <= c < FC + LAG and (c - LAG) % FJ == FJ - 1:
                    use_output((c - LAG) // FJ, f, role)

            def ffn(beside, f, role, m, before, attentions=None, unused=0, splits=False):
                if splits:
                    for b in range(blocks_before(1)):
                        split_block(b, order[b])
                for c in range(FC):
                    if splits and c % FJ == 0:
                        for b in range(blocks_before(c // FJ + 1), blocks_before(c // FJ + 2)):
                            split_block(b, order[b])
                    ffn_slot(c, f, role, unused)
                    if isinstance(before, dict) and c < TAIL:
                        ffn_slot(FC + c, **before)
                    if beside:
                        beside(c)

            def attention(a, m, beside, before, then):
                def rotate(w):
                    hp, j = divmod(w, 4)
                    dve.wait_ge(proj_made, UNITS * a + w + 1)
                    if j == 0:
                        wait(dve, q_ready, HP * a + hp)
                    if j == 2:
                        wait(dve, k_ready, HP * a + hp)
                    table = tables[:, j:j + 1, :].broadcast_to([P, 2, N // 2])
                    nc.vector.tensor_tensor(hidden[:, j, :].rearrange("p (b n) -> p b n", b=2),
                                            bank[w % 2][:].rearrange("p (b n) -> p b n", b=2), table,
                                            ALU.mult).then_inc(rot_mul, 1)

                def find_max(s):
                    dve.wait_ge(s_made, PAIRS * a + s + 1)
                    nc.vector.tensor_reduce(neg_max[:, s % 4, :], bank[2 + s % 2][:, 0:2 * KEYS].rearrange(
                        "p (h k) -> p h k", h=2), AX_X, ALU.max, negate=True).then_inc(max_ready, 1)

                def invert_sums(s):
                    dve.wait_ge(exp_done, 2 * (PAIRS * a + s + 1))
                    nc.vector.reciprocal(row_inv[:, s % 4, :], row_sum[:, s % 4, :]).then_inc(inv_ready, 1)

                def normalise_first(s):
                    dve.wait_ge(inv_ready, PAIRS * a + s + 1)
                    part = probs[s % PR][:, 0:KEYS]
                    nc.vector.tensor_scalar(part, part, row_inv[:, s % 4, 0:1], None, ALU.mult).then_inc(norm_done, 1)

                def persistent_parts(s):
                    return (probs[s % PR][:, PERSISTENT],
                            pm_parts[:, s % 2, :].rearrange("p (i k) -> p i k", i=3))

                def persistent_hi(s):
                    raw, parts = persistent_parts(s)
                    dve.wait_ge(norm_done, PAIRS * a + s + 1)
                    dve.wait_ge(norm_done_act, PAIRS * a + s + 1)
                    if s >= 2:
                        dve.wait_ge(t_made, PAIRS * a + s - 1)
                    nc.vector.tensor_copy(parts[:, 0:3:2, :], raw.unsqueeze(1).broadcast_to([P, 2, 2 * PM])).then_inc(parts_hi, 1)

                def persistent_lo(s):
                    raw, parts = persistent_parts(s)
                    dve.wait_ge(parts_hi, PAIRS * a + s + 1)
                    nc.vector.tensor_tensor(parts[:, 1, :], raw, parts[:, 0, :].bitcast(F32), ALU.subtract).then_inc(p_ready, 1)

                def output_low(hp):
                    dve.wait_ge(o_hi, HP * a + hp + 1)
                    nc.vector.tensor_tensor(h_lo[:, hp % 2, :], acc[:], h_hi[:, hp % 2, :].bitcast(F32),
                                            ALU.subtract).then_inc(o_lo, 1)

                for w in range(LEAD):
                    rotate(w)
                    if before and w < TAIL:
                        ffn_slot(FC + w, **before)
                for s in range(SLOTS):
                    if s < PAIRS:
                        find_max(s)
                    if 0 <= s - 1 < PAIRS:
                        normalise_first(s - 1)
                    if s + LEAD < UNITS:
                        rotate(s + LEAD)
                    if 0 <= s - 1 < PAIRS:
                        persistent_hi(s - 1)
                    if s < PAIRS:
                        invert_sums(s)
                    if 0 <= s - 1 < PAIRS:
                        persistent_lo(s - 1)
                    if s > O_LAG and (s - O_LAG - 1) % NT == 0 and (s - O_LAG - 1) // NT < HP:
                        output_low((s - O_LAG - 1) // NT)
                    beside(s)

            LINKS = 5

            def prep(slot, role, n, r, m, src, loads=None):
                for step in steps_of(slot, PREP):
                    if step == "stats":
                        if role == 0:
                            dve.wait_ge(ld_x, 16 * loads)
                        else:
                            dve.wait_ge(side_used, m)
                        for t in range(NT):
                            last = nc.vector.bn_stats(stats[:, t, :], src[:, t, :])
                        last.then_inc(norm_self, 1)
                    if step == "variance":
                        wait_apart(dve, (norm_self, n + 1))
                        for t in range(NT):
                            last = nc.vector.bn_aggr(mean_vars[role % 2][:, t, :], stats[:, t, :])
                        last.then_inc(stats_ready, 1)
                    if step in ("x_hat", "x_hat_rest"):
                        if step == "x_hat":
                            dve.wait_ge(rstd_ready, n + 1)
                        scale = 3 if role == 1 else 1
                        for t in range(NT // 2) if step == "x_hat" else range(NT // 2, NT):
                            last = nc.vector.tensor_scalar(x_hat[:, t, :], src[:, t, :], mean_vars[role % 2][:, t, 0:1],
                                                           rstd[:, scale, t:t + 1], ALU.subtract, ALU.mult)
                        if step == "x_hat_rest":
                            last.then_inc(xhat_ready, 1)
                    if step == "split":
                        dve.wait_ge(norm_hi_ready, n + 1)
                        high = norm_hi[role][:].bitcast(F32)
                        if role == 1:
                            nc.vector.scalar_tensor_tensor(norm_lo[role][:], side[:], g_col[:, 0:1], high,
                                                           ALU.mult, ALU.subtract).then_inc(side_used, 1)
                        else:
                            nc.vector.tensor_tensor(norm_lo[role][:], side[:], high, ALU.subtract).then_inc(side_used, 1)
                    if role == 1:
                        continue
                    def link(ins, done):
                        ins.then_inc(prep_self, 1)
                        dve.wait_ge(prep_self, LINKS * r + done)
                    if step == "copy":
                        dve.wait_ge(side_made, m + 2)
                        nc.vector.tensor_copy(logits[:], side[:, 0:NT * EXPERTS].rearrange(
                            "p (t e) -> p t e", t=NT)).then_inc(side_used, 1)
                    if step == "compare":
                        wait_apart(dve, (side_used, m + 2))
                        other = logits[:].unsqueeze(2).broadcast_to([P, NT, EXPERTS, EXPERTS])
                        own = logits[:].unsqueeze(3).broadcast_to([P, NT, EXPERTS, EXPERTS])
                        for t in range(NT):
                            last = nc.vector.max(top8[:, t, :], logits[:, t, :])
                        nc.vector.tensor_tensor(cmp_ge, other, own, ALU.is_ge)
                        link(nc.vector.tensor_tensor(cmp_gt, other, own, ALU.is_gt), 1)
                    if step == "ties":
                        tie = below[:].unsqueeze(1).broadcast_to([P, NT, EXPERTS, EXPERTS])
                        rest = above[:].unsqueeze(1).broadcast_to([P, NT, EXPERTS, EXPERTS])
                        nc.vector.tensor_tensor(cmp_ge, cmp_ge, tie, ALU.mult)
                        link(nc.vector.tensor_tensor(cmp_gt, cmp_gt, rest, ALU.mult), 2)
                    if step == "rank":
                        link(nc.vector.tensor_tensor(cmp_gt, cmp_gt, cmp_ge, ALU.add), 3)
                        link(nc.vector.tensor_reduce(rank[:], cmp_gt, AX_X, ALU.add), 4)
                    if step == "chosen":
                        nc.vector.tensor_scalar(rank[:], rank[:], 2.0, 0.25, ALU.is_lt, ALU.mult)
                        link(nc.vector.tensor_tensor(top_sum[:], top8[:, :, 0:1], top8[:, :, 1:2], ALU.add), 5)
                    if step == "centre":
                        nc.vector.scalar_tensor_tensor(centred[:], top_sum[:].broadcast_to([P, NT, EXPERTS]), -0.5,
                                                       logits[:], ALU.mult, ALU.add).then_inc(centred_ready, 1)
                    if step == "gates":
                        dve.wait_ge(tanh_ready, r + 1)
                        nc.vector.scalar_tensor_tensor(gates[:], tanhs[:], 1.0, rank[:], ALU.add,
                                                       ALU.mult).then_inc(gates_ready, 1)
                    if step == "gates_split":
                        dve.wait_ge(gates_hi_ready, r + 1)
                        part = gates_t[role // 2]
                        nc.vector.tensor_tensor(part[32:32 + EXPERTS, :], side[0:EXPERTS, :],
                                                part[0:EXPERTS, :].bitcast(F32), ALU.subtract).then_inc(side_used, 1)

            def finish(slot, role, m, count, g):
                for step in steps_of(slot, FINISH):
                    if step == "add":
                        dve.wait_ge(side_made, m + 1)
                        old, new = ((x1, x2), (x2, x3), (x3, x3))[role]
                        if role == 1:
                            wait(dve, st_out, 16 * g + 16)
                        nc.vector.tensor_tensor(new[:], side[:].rearrange("p (t d) -> p t d", t=NT), old[:],
                                                ALU.add).then_inc(side_used, 1)

            program(nc.vector, ffn_slot, ffn, attention, prep, finish, start)

        @block.gpsimd
        def _(pool):
            def start():
                done = [0]

                def link(ins):
                    done[0] += 1
                    ins.then_inc(pool_self, 1)
                    pool.wait_ge(pool_self, done[0])

                link(nc.gpsimd.memset(ident[:], 0.0))
                link(nc.gpsimd.memset(ident_bf[:], 0.0))
                link(nc.gpsimd.memset(mask_bf[:], 0.0))
                link(nc.gpsimd.memset(pick_raw[:], 0.0))
                for x in (ident, ident_bf):
                    link(nc.gpsimd.affine_select(out=x[:], in_=x[:], compare_op=ALU.not_equal, fill=1.0, base=0,
                                                 pattern=[[-1, P]], channel_multiplier=1))
                for at in OWN:
                    own = mask_bf[:, at:at + P]
                    link(nc.gpsimd.affine_select(out=own, in_=own, compare_op=ALU.is_ge, fill=MASKED, base=0,
                                                 pattern=[[-1, P]], channel_multiplier=1))
                    link(nc.gpsimd.memset(mask_bf[SEG:P, at:at + SEG], MASKED))
                pool.sem_inc(consts_pool, 1)
                for base in (0, -32):
                    last = nc.gpsimd.affine_select(out=pick_raw[:], in_=pick_raw[:], compare_op=ALU.not_equal,
                                                   fill=1.0, base=base, pattern=[[-1, EXPERTS]], channel_multiplier=1)
                    if base == 0:
                        link(last)
                last.then_inc(consts_pool, 1)
                nc.gpsimd.memset(minus_half[:], -0.5)
                for quarter, (first, second) in enumerate(((1.0, 0.0), (0.0, 1.0), (1.0, 0.0), (0.0, 1.0))):
                    rows = slice(quarter * 32, (quarter + 1) * 32)
                    link(nc.gpsimd.memset(head_rows[rows, 0:1], first))
                    link(nc.gpsimd.memset(head_rows[rows, 1:2], second))
                for i in range(2):
                    nc.gpsimd.memset(gates_t[i][:].bitcast(F32), 0.0)
                    nc.gpsimd.memset(k_diag[i][:], 0.0)
                nc.gpsimd.memset(below[:], 1.0)
                link(nc.gpsimd.memset(above[:], 1.0))
                for x, sign in ((below, 1), (above, -1)):
                    last = nc.gpsimd.affine_select(out=x[:], in_=x[:], compare_op=ALU.is_gt, fill=0.0, base=0,
                                                   pattern=[[sign, EXPERTS], [-sign, EXPERTS]], channel_multiplier=0)
                last.then_inc(consts_pool, 1)
                pool.wait_ge(consts_pool, 3)
                pool.wait_ge(ld_small, 16 * 4)

            def add_output(e, f):
                pool.wait_ge(y_used, FE * f + e + 1)
                if e >= 2:
                    pool.wait_ge(acc_added, EXPERTS * f + e - 1)
                nc.gpsimd.tensor_tensor(acc[:], acc[:], gated[e % 2], ALU.add).then_inc(acc_added, 1)

            def ffn_slot(c, f, role, unused=0):
                if c < FC and c % 2 == 0:
                    wait_apart(pool, (hid_silu, FC * f + unused + c + 1), (down_done, FC * f + c - HR + 1))
                    nc.gpsimd.tensor_scalar(h_hi[:, c % HR, :], hidden[:, c % SR, :], 1.0, 1.0,
                                            ALU.mult, ALU.mult).then_inc(hid_hi_pool, 1)
                d = c - LAG - 1
                if d >= 2 * FJ - 1 and d % FJ == FJ - 1:
                    add_output(d // FJ, f)

            def ffn(beside, f, role, m, before, attentions=None, unused=0, splits=False):
                for c in range(FC):
                    ffn_slot(c, f, role, unused)
                    if isinstance(before, dict) and c < TAIL:
                        ffn_slot(FC + c, **before)
                    if beside:
                        beside(c)

            def attention(a, m, beside, before, then):
                def add_products(w):
                    hp, j = divmod(w, 4)
                    if j == 1:
                        pool.wait_ge(rot_mul, UNITS * a + w + 1)
                        if hp >= 2:
                            pool.wait_ge(s_made, PAIRS * a + NT * (hp - 1))
                        nc.gpsimd.tensor_tensor(q_rot[hp % 2], hidden[:, 0, :], hidden[:, 1, :],
                                                ALU.add).then_inc(q_ready, 1)
                    if j == 3:
                        pool.wait_ge(rot_mul, UNITS * a + w + 1)
                        if hp >= 2:
                            pool.wait_ge(s_made, PAIRS * a + NT * (hp - 1))
                        nc.gpsimd.tensor_tensor(hidden[:, 2, :], hidden[:, 2, :], hidden[:, 3, :],
                                                ALU.add).then_inc(k_added, 1)
                        wait_apart(pool, (k_added, HP * a + hp + 1))
                        for h in range(2):
                            nc.gpsimd.tensor_scalar(k_diag[hp % 2][:, :, OWN[h]:OWN[h] + P],
                                                    hidden[:, 2, :].rearrange("p (t n) -> p t n", t=NT),
                                                    head_rows[:, h:h + 1], 1.0, ALU.mult, ALU.mult)
                        nc.gpsimd.tensor_scalar(k_diag[hp % 2][:, :, PERSISTENT],
                                                pmk_sb[:, hp:hp + 1, :].broadcast_to([P, NT, 2 * PM]),
                                                1.0, 1.0, ALU.mult, ALU.mult).then_inc(k_ready, 1)

                def output_hi(hp):
                    waits = [(o_raw, HP * a + hp + 1)]
                    if hp >= 2:
                        waits.append((wout_done, HP * a + hp - 1))
                    wait_apart(pool, *waits)
                    nc.gpsimd.tensor_scalar(h_hi[:, hp % 2, :], acc[:], 1.0, 1.0, ALU.mult, ALU.mult).then_inc(o_hi, 1)

                if before:
                    for c in range(FC, FC + TAIL):
                        ffn_slot(c, **before)
                for w in range(LEAD):
                    add_products(w)
                for s in range(SLOTS):
                    if s >= O_LAG and (s - O_LAG) % NT == 0 and (s - O_LAG) // NT < HP:
                        output_hi((s - O_LAG) // NT)
                    if s + LEAD < UNITS:
                        add_products(s + LEAD)
                    beside(s)

            LINKS = 5

            def prep(slot, role, n, r, m, src, loads=None):
                for step in steps_of(slot, PREP):
                    def link(ins, done):
                        ins.then_inc(rms_self, 1)
                        wait_apart(pool, (rms_self, LINKS * r + done))
                    if step == "rstd":
                        wait_apart(pool, (stats_ready, n + 1))
                        nc.gpsimd.tensor_scalar(rstd[:, 0, :], mean_vars[role % 2][:, :, 1], 1.0, LN_EPS,
                                                ALU.mult, ALU.add).then_inc(rstd_self, 1)
                        wait_apart(pool, (rstd_self, n + 1))
                        last = nc.gpsimd.tensor_tensor(rstd[:, 1, :], rstd[:, 0, :], minus_half[:], ALU.pow)
                        if role == 1:
                            link(last, 1)
                        else:
                            last.then_inc(rstd_ready, 1)
                    if step == "rms" and role == 1:
                        link(nc.gpsimd.tensor_tensor(rstd[:, 2, :], rstd[:, 1, :], rstd[:, 1, :], ALU.mult), 2)
                        link(nc.gpsimd.tensor_tensor(rstd[:, 2, :], rstd[:, 2, :], mean_vars[role % 2][:, :, 1], ALU.mult), 3)
                        link(nc.gpsimd.tensor_scalar(rstd[:, 2, :], rstd[:, 2, :], 1.0, RMS_EPS, ALU.mult, ALU.add), 4)
                    if step == "rms_rstd" and role == 1:
                        link(nc.gpsimd.tensor_tensor(rstd[:, 3, :], rstd[:, 2, :], minus_half[:], ALU.pow), 5)
                        nc.gpsimd.tensor_tensor(rstd[:, 3, :], rstd[:, 3, :], rstd[:, 1, :], ALU.mult).then_inc(rstd_ready, 1)

            def finish(slot, role, m, count, g):
                pass

            program(nc.gpsimd, ffn_slot, ffn, attention, prep, finish, start)


def stage(values, slot):
    return values[:, slot // 2, slot % 2 * N:(slot % 2 + 1) * N]


def x_hat_stage(values):
    return values[0:96, NT - 1, :].rearrange("p (h d) -> p h d", h=HP)


def blocks_before(experts):
    rest = BLOCKS - Q_AT
    experts = min(experts, FE)
    return 2 * experts + (rest * (experts - 1) + FE - 2) // (FE - 1)


def split_order():
    order = []
    for e in range(FE):
        order += [2 * e, 2 * e + 1]
        while len(order) < blocks_before(e + 1):
            order.append(Q_AT + len(order) - 2 * (e + 1))
    return order


def kernel(L0_attn_seq, L0_attn_g_norm, L0_attn_W_qkv, L0_attn_W_out, L0_attn_pm,
           L0_ffn_shared_w1, L0_ffn_shared_w2, L0_ffn_experts_w1, L0_ffn_experts_w2, L0_ffn_gate_w):
    import numpy as np
    import concourse.bacc as bacc
    from concourse import mybir as mb
    from concourse.bass_utils import run_bass_kernel_spmd

    seq, wqkv, wout, pm = (np.asarray(a) for a in (L0_attn_seq, L0_attn_W_qkv, L0_attn_W_out, L0_attn_pm))
    b, s, d = seq.shape
    groups = b * s // N
    x = seq.reshape(groups, NT, P, d).transpose(0, 2, 1, 3)
    shape = x.shape
    x = np.concatenate([x, x[:1]])

    half = np.arange(DH // 2)
    channel = np.concatenate([2 * half, 2 * half, 2 * half + 1, 2 * half + 1])
    head = np.repeat([0, 1, 0, 1], DH // 2)
    cols = (np.arange(HP)[:, None] * 2 + head) * DH + channel
    cols = np.concatenate([cols, cols[:, :DH]], axis=1).reshape(-1)
    inner = HEADS * DH
    w1 = np.concatenate([np.asarray(L0_ffn_shared_w1)[None], np.asarray(L0_ffn_experts_w1)])
    w2 = np.concatenate([np.asarray(L0_ffn_shared_w2)[None], np.asarray(L0_ffn_experts_w2)])
    w1 = w1.transpose(2, 0, 1)
    w2 = w2.reshape(FE, d, FJ, P).transpose(3, 0, 2, 1).reshape(P, FE, FJ * d)
    experts = np.stack([w1, w2], axis=2).reshape(P, -1)
    weights = np.concatenate([experts, wqkv[:, cols], wqkv[:, inner + cols], wqkv[:, 2 * inner:],
                              wout.reshape(HP, P, d).transpose(1, 0, 2).reshape(P, -1)], axis=1)

    pm_k = np.zeros((P, HP, 2, PM), pm.dtype)
    pm_v = np.zeros((3, 2, PM, HP, 2, DH), pm.dtype)
    for h in range(2):
        pm_k[head == h, :, h, :] = pm[0, h::2][:, :, channel[head == h]].transpose(2, 0, 1)
        pm_v[:, h, :, :, h, :] = pm[1, h::2].transpose(1, 0, 2)
    pm_k, pm_v = pm_k.reshape(P, HP, 2 * PM), pm_v.reshape(96, HP, P)

    freq = np.float32(1) / np.float32(10000.0) ** (np.arange(0, DH, 2, dtype=np.float32) / np.float32(DH))
    angle = (np.arange(s, dtype=np.float32)[:, None] * freq).T.astype(np.float32)
    angle = angle[channel // 2]
    cos, sin = np.cos(angle), np.where(channel[:, None] % 2, np.sin(angle), -np.sin(angle))
    rotary = np.stack([cos * DH ** -0.5, sin * DH ** -0.5, cos, sin], axis=1).astype(np.float32)

    ins = {"x": x, "weights": weights, "gate_w": np.asarray(L0_ffn_gate_w).T, "g_norm": np.asarray(L0_attn_g_norm)[:, None],
           "pm_k": pm_k, "pm_v": pm_v, "rotary": rotary}
    nc = bacc.Bacc("TRN2", target_bir_lowering=False, num_devices=1)
    arrays, args = {}, []
    for name, a in ins.items():
        arrays[name] = np.ascontiguousarray(a)
        args.append(nc.dram_tensor(name, a.shape, mb.dt.from_np(a.dtype), kind="ExternalInput").ap())
    args.append(nc.dram_tensor("out", shape, mb.dt.float32, kind="ExternalOutput").ap())
    macaron(nc, *args)
    r = run_bass_kernel_spmd(nc, [arrays], core_ids=[0])
    out = np.asarray(r.results[0]["out"])
    return out.transpose(0, 2, 1, 3).reshape(b, s, d)
```

```python
from contextlib import ExitStack

import concourse.bass as bass
from concourse import mybir

F32 = mybir.dt.float32
F32R = mybir.dt.float32r
BF16 = mybir.dt.bfloat16
ALU = mybir.AluOpType
ACT = mybir.ActivationFunctionType
AX_X = mybir.AxisListType.X

P = 128
N = 512
NT = N // P
HEADS, DH, SEG, PM = 16, 64, 64, 16
HP = HEADS // 2
PAIRS = HP * NT
KEYS = P + PM
OWN = (0, P + 2 * PM)
PERSISTENT = slice(P, P + 2 * PM)
EXPERTS = 8
FE = 1 + EXPERTS
FJ = 4
FC = FE * FJ
LN_EPS = 1e-5
RMS_EPS = 2.0 ** -23
MASKED = -1e30

QK_COLS = 3 * DH
Q_AT = 2 * FE
K_AT = Q_AT + HP * QK_COLS // N
V_AT = K_AT + HP * QK_COLS // N
OUT_AT = V_AT + 2
BLOCKS = OUT_AT + 2
STAGES = 6
AHEAD = 2
LAG = 3
ACT_HI, POOL_HI = (0, 3), (1, 2)
GATES_AT = 3
SR = 4
HR = 3
OUTPUT_SLOT = (0, 2)
PR = 3
LEAD = 6
UNITS = 4 * HP
TAIL = LAG + 1
HEAD = 4
BEGUN = 7
T_LAG, AV_LAG = 2, 3
O_LAG = NT - 1 + AV_LAG
W_LAG = O_LAG + 3
ACT_NORMS = UNITS - LEAD
SLOTS = NT * (HP - 1) + W_LAG + 1

PREP = {"stats": 0, "variance": 1, "rstd": 5, "x_hat": 6, "x_hat_rest": 7, "transpose": 10, "split": 10,
        "logits": 14, "copy": 14, "compare": 15, "ties": 16, "rank": 17, "chosen": 18, "centre": 18,
        "tanh": 20, "gates": 20, "gates_t": 24, "gates_split": 24}
LATE = 34
ROWS = range(PREP["logits"])
PREP_END = PREP["gates_split"] + 1
KEEP_BUSY = {"stats": 18, "split": 4}
KEEP_BUSY_FIRST = {"stats": 22, "split": 8}
FINISH = {"transpose": 0, "add": 0}


def macaron(nc, x_in, weights, gate_w, g_norm, pm_k, pm_v, rotary, x_out):
    groups = x_in.shape[0] - 1
    ctx = ExitStack()
    with ctx:
        def sb(name, shape, dt=F32):
            return ctx.enter_context(nc.sbuf_tensor(name, shape, dt))

        def sem(name):
            return ctx.enter_context(nc.semaphore(name))

        w_hi = sb("w_hi", [P, BLOCKS * N], F32R)
        w_lo = sb("w_lo", [P, BLOCKS * N], F32R)
        values = sb("values", [P, NT, HEADS * DH])
        k_diag = [sb(f"k_diag{i}", [P, NT, 2 * KEYS]) for i in range(2)]
        hidden = sb("hidden", [P, SR, N])
        h_hi = sb("h_hi", [P, HR, N], F32R)
        h_lo = sb("h_lo", [P, HR, N], F32R)
        scratch = sb("scratch", [P, 4 * N])
        gate_cols = [scratch[:, i * N:(i + 1) * N] for i in range(2)]
        gated = [scratch[:, (2 + i) * N:(3 + i) * N] for i in range(2)]
        q_rot = [scratch[:, i * N:(i + 1) * N] for i in range(2)]
        probs = [scratch[:, 2 * N + i * 2 * KEYS:2 * N + (i + 1) * 2 * KEYS]
                 for i in range(PR)]
        probs_t = sb("probs_t", [P, 2, 2 * P])
        pm_t = [x[0:6 * PM, 1, :] for x in (h_hi, h_lo)]
        pm_parts = sb("pm_parts", [P, 2, 6 * PM], F32R)
        norm_hi = [sb(f"norm_hi{i}", [P, N], F32R) for i in range(3)]
        norm_lo = [sb(f"norm_lo{i}", [P, N], F32R) for i in range(3)]
        gates_t = [sb(f"gates_t{i}", [DH, N], F32R) for i in range(2)]
        x1 = sb("x1", [P, NT, P])
        x2 = sb("x2", [P, NT, P])
        x3 = sb("x3", [P, NT, P])
        x_hat = sb("x_hat", [P, NT, P])
        acc = sb("acc", [P, N])
        tables = sb("tables", [P, 4, N // 2])
        ident = sb("ident", [P, P])
        ident_bf = sb("ident_bf", [P, P], BF16)
        mask_bf = sb("mask_bf", [P, 2 * KEYS], BF16)
        gate_raw = sb("gate_raw", [P, EXPERTS])
        gate_hi = sb("gate_hi", [P, EXPERTS], F32R)
        gate_lo = sb("gate_lo", [P, EXPERTS], F32R)
        pick_raw = sb("pick_raw", [DH, EXPERTS])
        pick = sb("pick", [DH, EXPERTS], F32R)
        below = sb("below", [P, EXPERTS, EXPERTS])
        above = sb("above", [P, EXPERTS, EXPERTS])
        head_rows = sb("head_rows", [P, 2])
        g_col = sb("g_col", [P, 1])
        pmk_sb = sb("pmk_sb", [P, HP, 2 * PM])
        pmv_sb = sb("pmv_sb", [96, HP, P], F32R)
        stats = sb("stats", [P, NT, 6])
        mean_vars = [sb(f"mean_var{i}", [P, NT, 2]) for i in range(2)]
        rstd = sb("rstd", [P, 2, NT])
        minus_half = sb("minus_half", [P, NT])
        logits = sb("logits", [P, NT, EXPERTS])
        top8 = sb("top8", [P, NT, EXPERTS])
        cmp_ge, cmp_gt = (x_hat[:, i:i + NT // 2, :].rearrange("p a (b e j) -> p (a b) e j", e=EXPERTS, j=EXPERTS)
                          for i in (0, NT // 2))
        rank = sb("rank", [P, NT, EXPERTS])
        top_sum = sb("top_sum", [P, NT, 1])
        centred = sb("centred", [P, NT, EXPERTS])
        tanhs = sb("tanhs", [P, NT, EXPERTS])
        gates = sb("gates", [P, NT, EXPERTS])
        neg_max = sb("neg_max", [P, 4, 2])
        row_sum = sb("row_sum", [P, 4, 2])
        row_inv = sb("row_inv", [P, 4, 2])
        warm = sb("warm", [P, 1])

        bank = [ctx.enter_context(nc.psum_tensor(f"bank{i}", [P, N], F32)) for i in range(8)]
        side = bank[7]
        v_bank = (bank[2], bank[3], bank[6])

        ld_x, ld_gate, ld_small, ld_pmv, st_out = sem("ld_x"), sem("ld_gate"), sem("ld_small"), sem("ld_pmv"), sem("st_out")
        ld_w = [sem(f"ld_w{i}") for i in range(STAGES)]
        split_hi, split_lo = sem("split_hi"), sem("split_lo")
        consts_pool, consts_act, consts_dve, pool_self = sem("consts_pool"), sem("consts_act"), sem("consts_dve"), sem("pool_self")
        hid_made, hid_silu, hid_hi_act, hid_hi_pool, hid_lo = (
            sem("hid_made"), sem("hid_silu"), sem("hid_hi_act"), sem("hid_hi_pool"), sem("hid_lo"))
        down_done, y_used, gcols_made, gcols_copied, acc_added = (
            sem("down_done"), sem("y_used"), sem("gcols_made"), sem("gcols_copied"), sem("acc_added"))
        side_made, side_used = sem("side_made"), sem("side_used")
        passed = sem("passed")
        stats_ready, rstd_ready, xhat_ready, norm_hi_ready = (
            sem("stats_ready"), sem("rstd_ready"), sem("xhat_ready"), sem("norm_hi_ready"))
        prep_self, norm_self, centred_ready, tanh_ready, gates_ready, gates_hi_ready = (
            sem("prep_self"), sem("norm_self"), sem("centred_ready"), sem("tanh_ready"), sem("gates_ready"), sem("gates_hi_ready"))
        v_made, v_copied, proj_made, rot_mul, q_ready, k_ready, k_added, rstd_self = (
            sem("v_made"), sem("v_copied"), sem("proj_made"), sem("rot_mul"), sem("q_ready"), sem("k_ready"),
            sem("k_added"), sem("rstd_self"))
        norm_done_act, parts_hi, o_raw = sem("norm_done_act"), sem("parts_hi"), sem("o_raw")
        s_made, max_ready, exp_done, inv_ready, p_ready = (
            sem("s_made"), sem("max_ready"), sem("exp_done"), sem("inv_ready"), sem("p_ready"))
        t_made, t_copied, norm_done, av_done = (
            sem("t_made"), sem("t_copied"), sem("norm_done"), sem("av_done"))
        o_hi, o_lo, wout_done, yatt_copied = sem("o_hi"), sem("o_lo"), sem("wout_done"), sem("yatt_copied")

        def w1(part, e, j):
            return part[:, 2 * e * N + j * P:2 * e * N + (j + 1) * P]

        def w2(part, e, j):
            return part[:, (2 * e + 1) * N + j * P:(2 * e + 1) * N + (j + 1) * P]

        def y_bank(e, f, role):
            odd = f % 2 if isinstance(f, int) else 1 - role // 2
            return bank[4 + (e + odd) % 2][:]

        def wait(eng, s, value):
            if not isinstance(value, int) or value > 0:
                eng.wait_ge(s, value)

        def wait_apart(eng, *waits):
            for s, v in waits:
                wait(eng, s, v)
            eng.sem_inc(passed, 1)

        def program(eng, ffn_slot, ffn, attention, prep, finish, start):
            start()
            def routing(slot):
                at = PREP["logits"] + 2 * slot
                return range(at, at + 2) if slot < 4 else range(PREP["gates_t"], PREP_END) if slot == 5 else range(0)

            prep(ROWS, role=0, n=0, r=0, m=0, src=x1, loads=1)

            def beside_lead_in(slot):
                prep(routing(slot), role=0, n=0, r=0, m=0, src=x1, loads=1)
            ffn(beside_lead_in, f=0, role=0, m=0, before=None, splits=True)
            for c in range(FC, FC + TAIL):
                ffn_slot(c, f=0, role=0)
            finish(None, role=0, m=3, count=0, g=0)
            prep(None, role=1, n=1, r=0, m=4, src=x2)

            def beside_first_attention(slot):
                prep(slot - 3, role=0, n=2, r=1, m=5, src=x1, loads=2)
            attention(a=0, m=4, beside=beside_first_attention, before=None, then=dict(f=1, role=0, m=5))

            with eng.Fori(0, groups - 1) as g:
                def beside_first_ffn(slot):
                    finish(slot - 4, role=1, m=10 * g + 8, count=g, g=g)
                    prep(slot - 7, role=2, n=3 * g + 3, r=2 * g + 2, m=10 * g + 9, src=x3)
                ffn(beside_first_ffn, f=2 * g + 1, role=0, m=10 * g + 5, before="attention", attentions=g + 1)

                def beside_second_ffn(slot):
                    finish(slot - 5, role=0, m=10 * g + 12, count=2 * g + 1, g=g)
                    prep(slot - 7, role=1, n=3 * g + 4, r=g + 1, m=10 * g + 13, src=x2)
                    prep(slot - 11, role=0, n=3 * g + 5, r=2 * g + 3, m=10 * g + 14, src=x1, loads=g + 3)
                ffn(beside_second_ffn, f=2 * g + 2, role=2, m=10 * g + 9, before=dict(f=2 * g + 1, role=0))

                def beside_attention(slot):
                    finish(slot - 4, role=2, m=10 * g + 17, count=2 * g + 2, g=g)
                attention(a=g + 1, m=10 * g + 13, beside=beside_attention, before=dict(f=2 * g + 2, role=2),
                          then=dict(f=2 * g + 3, role=0, m=10 * g + 14))

            g = groups - 1
            finish(None, role=1, m=10 * g + 8, count=g, g=g)
            prep(ROWS, role=2, n=3 * g + 3, r=2 * g + 2, m=10 * g + 9, src=x3)

            def beside_last_ffn(slot):
                prep(routing(slot), role=2, n=3 * g + 3, r=2 * g + 2, m=10 * g + 9, src=x3)
            ffn(beside_last_ffn, f=2 * g + 1, role=2, m=10 * g + 9, before=None, unused=HEAD)
            for c in range(FC, FC + TAIL):
                ffn_slot(c, f=2 * g + 1, role=2, unused=HEAD)
            finish(None, role=2, m=10 * g + 12, count=2 * g + 1, g=g)

        def steps_of(slot, schedule):
            slots = range(PREP_END) if slot is None else slot if isinstance(slot, range) else [slot]
            return [step for step, at in schedule.items() if at in slots]

        block = ctx.enter_context(nc.Block())

        @block.sync
        def _(sp):
            sp.sem_inc(st_out, 16)
            sp.dma_start(x1[:], x_in[0]).then_inc(ld_x, 16)
            sp.dma_start(gate_raw[:], gate_w).then_inc(ld_gate, 16)
            for b, blk in enumerate(split_order()):
                slot = b % STAGES
                if b == blocks_before(1):
                    sp.dma_start(pmv_stage(values), pm_v).then_inc(ld_pmv, 16)
                    for dst, src in ((g_col[:], g_norm), (pmk_sb[:], pm_k), (tables[:], rotary)):
                        sp.dma_start(dst, src).then_inc(ld_small, 16)
                if b >= STAGES:
                    sp.wait_ge(split_lo, b - STAGES + 1)
                sp.dma_start(stage(values, slot), weights[:, blk * N:(blk + 1) * N]).then_inc(ld_w[slot], 16)
            sp.wait_ge(side_used, 4)
            sp.dma_start(x1[:], x_in[1]).then_inc(ld_x, 16)
            with sp.Fori(0, groups - 1) as g:
                wait_apart(sp, (side_used, 10 * g + 13))
                sp.dma_start(x1[:], x_in[2:][g]).then_inc(ld_x, 16)
                wait_apart(sp, (side_used, 10 * g + 18))
                sp.dma_start(x_out[g], x3[:]).then_inc(st_out, 16)
            sp.wait_ge(side_used, 10 * (groups - 1) + 13)
            sp.dma_start(x_out[groups - 1], x3[:]).then_inc(st_out, 16)
            sp.wait_ge(st_out, 16 * (groups + 1))
            sp.wait_ge(ld_x, 16 * (groups + 1))

        @block.tensor
        def _(pe):
            def split3(out, lhs_hi, lhs_lo, rhs_hi, rhs_lo, start, stop):
                nc.tensor.matmul(out, lhs_hi, rhs_hi, start=start, stop=False)
                nc.tensor.matmul(out, lhs_hi, rhs_lo, start=False, stop=False)
                return nc.tensor.matmul(out, lhs_lo, rhs_hi, start=False, stop=stop)

            def start():
                pe.wait_ge(consts_pool, 1)

            def first_product(c, f, role, m, unused=0):
                if c == 0:
                    pe.wait_ge(side_used, m + 1)
                e, j = divmod(c, FJ)
                wait(pe, hid_silu, FC * f + unused + c - 3)
                split3(bank[c % 4][:], w1(w_hi, e, j), w1(w_lo, e, j), norm_hi[role][:],
                       norm_lo[role][:], True, True).then_inc(hid_made, 1)

            def spread_gates(e, f, role, m, attentions):
                if e == 1:
                    pe.wait_ge(side_used, m + 3)
                    if attentions is not None:
                        pe.wait_ge(yatt_copied, attentions)
                wait(pe, gcols_copied, EXPERTS * f + e - 1)
                nc.tensor.matmul(bank[6][:], pick[:, e - 1:e].broadcast_to([DH, P]),
                                 gates_t[role // 2][:], start=True, stop=True).then_inc(gcols_made, 1)

            def ffn_slot(c, f, role, m=None, begun=0, attentions=None, unused=0, splits=False):
                if splits and c < FC and c % FJ == 0:
                    pe.wait_ge(split_lo, blocks_before(c // FJ + 1))
                if FJ <= c < FC and c % FJ == GATES_AT:
                    spread_gates(c // FJ, f, role, m, attentions)
                if begun <= c < FC:
                    first_product(c, f, role, m, unused)
                if LAG <= c < FC + LAG:
                    d = c - LAG
                    e, j = divmod(d, FJ)
                    if j == 0:
                        wait(pe, y_used, FE * f + e - 1)
                    pe.wait_ge(hid_lo, FC * f + d + 1)
                    split3(y_bank(e, f, role), w2(w_hi, e, j), w2(w_lo, e, j), h_hi[:, d % HR, :],
                           h_lo[:, d % HR, :], j == 0, j == FJ - 1).then_inc(down_done, 1)

            def ffn(beside, f, role, m, before, attentions=None, unused=0, splits=False):
                for c in range(FC):
                    ffn_slot(c, f, role, m, BEGUN if before == "attention" else 0, attentions, unused, splits)
                    if isinstance(before, dict) and c < TAIL:
                        ffn_slot(FC + c, **before)
                    if beside:
                        beside(c)

            def attention(a, m, beside, before, then):
                xh, xl = norm_hi[1], norm_lo[1]
                pe.wait_ge(side_used, m + 1)
                if isinstance(a, int):
                    pe.wait_ge(split_lo, BLOCKS)
                    pe.wait_ge(consts_pool, 3)
                    pe.wait_ge(consts_dve, 2)
                def values_unit(v):
                    t, half = divmod(v, 2)
                    if v >= 3:
                        pe.wait_ge(v_copied, 2 * NT * a + v - 2)
                    elif before and v == 2:
                        pe.wait_ge(gcols_copied, EXPERTS * (before["f"] + 1))
                    cols = slice((V_AT + half) * N, (V_AT + half + 1) * N)
                    rows = slice(t * P, (t + 1) * P)
                    split3(v_bank[v % 3][:], xh[:, rows], xl[:, rows], w_hi[:, cols], w_lo[:, cols],
                           True, True).then_inc(v_made, 1)

                def project(w):
                    hp, j = divmod(w, 4)
                    if w >= 2:
                        pe.wait_ge(rot_mul, UNITS * a + w - 1)
                    at = (Q_AT, K_AT)[j // 2] * N + hp * QK_COLS + j % 2 * DH
                    parts = [x[:, at:at + P] for x in (w_hi, w_lo)]
                    split3(bank[w % 2][:], *parts, xh[:], xl[:], True, True).then_inc(proj_made, 1)

                def scores(s):
                    hp, p = divmod(s, NT)
                    if p == 0:
                        pe.wait_ge(q_ready, HP * a + hp + 1)
                        pe.wait_ge(k_ready, HP * a + hp + 1)
                    if s >= 2:
                        pe.wait_ge(exp_done, 2 * (PAIRS * a + s - 1))
                    else:
                        pe.wait_ge(v_copied, 2 * NT * (a + 1) - 1 + s)
                    out = bank[2 + s % 2][:, 0:2 * KEYS]
                    nc.tensor.matmul(out, ident_bf[:], mask_bf[:], start=True, stop=False)
                    nc.tensor.matmul(out, q_rot[hp % 2][:, p * P:(p + 1) * P],
                                     k_diag[hp % 2][:, p], start=False, stop=True).then_inc(s_made, 1)

                def transpose(s):
                    pe.wait_ge(p_ready, PAIRS * a + s + 1)
                    if s >= 1:
                        pe.wait_ge(t_copied, PAIRS * a + s)
                    for h in range(2):
                        nc.tensor.transpose(bank[4][:, h * P:(h + 1) * P], probs[s % PR][:, OWN[h]:OWN[h] + P], ident[:])
                    nc.tensor.transpose(bank[4][0:6 * PM, 2 * P:3 * P], pm_parts[:, s % 2, :].bitcast(F32),
                                        ident[:]).then_inc(t_made, 1)

                def weigh_values(s):
                    hp, p = divmod(s, NT)
                    pe.wait_ge(t_copied, PAIRS * a + s + 1)
                    if p == 0 and hp >= 1:
                        pe.wait_ge(o_raw, HP * a + hp)
                    for h in range(2):
                        head = slice((2 * hp + h) * DH, (2 * hp + h + 1) * DH)
                        last = nc.tensor.matmul(bank[5][h * DH:(h + 1) * DH, p * P:(p + 1) * P],
                                                values[:, p, head], probs_t[:, s % 2, h * P:(h + 1) * P],
                                                start=p == 0, stop=False, skip_group_check=True)
                    if p == NT - 1:
                        last = nc.tensor.matmul(bank[5][:], pmv_sb[:, hp, :], pm_t[hp % 2][:],
                                                start=False, stop=True, skip_group_check=True)
                    last.then_inc(av_done, 1)

                def times_w_out(hp):
                    pe.wait_ge(o_lo, HP * a + hp + 1)
                    cols = slice(OUT_AT * N + hp * P, OUT_AT * N + (hp + 1) * P)
                    split3(bank[6][:], w_hi[:, cols], w_lo[:, cols], h_hi[:, OUTPUT_SLOT[hp % 2], :], h_lo[:, OUTPUT_SLOT[hp % 2], :],
                           hp == 0, hp == HP - 1).then_inc(wout_done, 1)

                if before:
                    pe.wait_ge(hid_silu, FC * (before["f"] + 1))
                for v in range(2 * NT):
                    if v < 2:
                        project(v)
                    values_unit(v)
                    if before and v < TAIL:
                        ffn_slot(FC + v, **before)
                    if 2 <= v < LEAD:
                        project(v)
                for s in range(SLOTS):
                    if s < PAIRS:
                        scores(s)
                    if s + LEAD < UNITS:
                        project(s + LEAD)
                    if s >= SLOTS - BEGUN:
                        first_product(s - (SLOTS - BEGUN), **then)
                    if 0 <= s - T_LAG < PAIRS:
                        transpose(s - T_LAG)
                    if 0 <= s - AV_LAG < PAIRS:
                        weigh_values(s - AV_LAG)
                    if s >= W_LAG and (s - W_LAG) % NT == 0:
                        times_w_out((s - W_LAG) // NT)
                    beside(s)

            def keep_busy(times):
                for _ in range(times):
                    nc.tensor.matmul(bank[6][:, 0:P], ident[:], ident[:], start=True, stop=True)

            def prep(slot, role, n, r, m, src, loads=None):
                alone = slot is None or slot is ROWS
                for step in steps_of(slot, PREP):
                    if alone and step in KEEP_BUSY:
                        first = isinstance(n, int) and n == 0
                        keep_busy((KEEP_BUSY_FIRST if first else KEEP_BUSY)[step])
                    if step == "transpose":
                        pe.wait_ge(xhat_ready, n + 1)
                        wait(pe, side_used, m)
                        for t in range(NT):
                            last = nc.tensor.transpose(side[:, t * P:(t + 1) * P], x_hat[:, t, :], ident[:])
                        last.then_inc(side_made, 1)
                    if step == "logits" and role != 1:
                        pe.wait_ge(side_used, m + 1)
                        if isinstance(n, int):
                            pe.wait_ge(consts_dve, 1)
                        for t in range(NT):
                            rows = slice(t * P, (t + 1) * P)
                            last = split3(side[:, t * EXPERTS:(t + 1) * EXPERTS], norm_hi[role][:, rows],
                                          norm_lo[role][:, rows], gate_hi[:], gate_lo[:], True, True)
                        last.then_inc(side_made, 1)
                    if step == "gates_t" and role != 1:
                        pe.wait_ge(gates_ready, r + 1)
                        pe.wait_ge(side_used, m + 2)
                        for t in range(NT):
                            last = nc.tensor.transpose(side[0:EXPERTS, t * P:(t + 1) * P], gates[:, t, :], ident[:])
                        last.then_inc(side_made, 1)

            def finish(slot, role, m, count, g):
                for step in steps_of(slot, FINISH):
                    if step == "transpose":
                        if role == 1:
                            pe.wait_ge(yatt_copied, count + 1)
                        else:
                            pe.wait_ge(acc_added, EXPERTS * (count + 1))
                        pe.wait_ge(side_used, m)
                        for t in range(NT):
                            last = nc.tensor.transpose(side[:, t * P:(t + 1) * P], acc[:, t * P:(t + 1) * P], ident[:])
                        last.then_inc(side_made, 1)

            program(nc.tensor, ffn_slot, ffn, attention, prep, finish, start)

        @block.scalar
        def _(act):
            def split_block(b, blk):
                slot = b % STAGES
                act.wait_ge(ld_w[slot], 16 * (b // STAGES + 1))
                nc.scalar.activation(w_hi[:, blk * N:(blk + 1) * N], stage(values, slot), ACT.Copy).then_inc(split_hi, 1)

            order = split_order()

            def start():
                for b in range(blocks_before(1) + AHEAD):
                    split_block(b, order[b])
                act.wait_ge(ld_gate, 16)
                nc.scalar.activation(gate_hi[:], gate_raw[:], ACT.Copy).then_inc(consts_act, 1)
                act.wait_ge(consts_pool, 2)
                nc.scalar.activation(pick[:], pick_raw[:], ACT.Copy)
                act.wait_ge(ld_small, 16 * 3)

            def silu(c, f, role, unused=0):
                act.wait_ge(hid_made, FC * f + (BEGUN if unused else 0) + c + 1)
                wait(act, hid_lo, FC * f + c - SR + 1)
                nc.scalar.activation(hidden[:, c % SR, :], bank[c % 4][:], ACT.Silu).then_inc(hid_silu, 1)

            def hidden_hi(d, f, unused=0):
                act.wait_ge(hid_silu, FC * f + unused + d + 1)
                nc.scalar.activation(h_hi[:, d % HR, :], hidden[:, d % SR, :], ACT.Copy).then_inc(hid_hi_act, 1)

            def ffn_slot(c, f, role, begun=0, unused=0):
                if begun <= c < FC:
                    silu(c, f, role, unused)
                d = c - 1
                if (1 if begun else 0) <= d < FC and d % FJ in ACT_HI:
                    wait(act, down_done, FC * f + d - HR + 1)
                    hidden_hi(d, f, unused)
                if FJ <= c < FC and c % FJ == GATES_AT:
                    e = c // FJ
                    act.wait_ge(gcols_made, EXPERTS * f + e)
                    wait(act, y_used, FE * f + e - 1)
                    nc.scalar.activation(gate_cols[e % 2], bank[6][:], ACT.Copy).then_inc(gcols_copied, 1)

            def ffn(beside, f, role, m, before, attentions=None, unused=0, splits=False):
                for c in range(FC):
                    if splits and split_at(c) is not None:
                        split_block(split_at(c), order[split_at(c)])
                    elif splits and c == LATE:
                        act.wait_ge(ld_pmv, 16)
                        nc.scalar.activation(pmv_sb[:], pmv_stage(values), ACT.Copy).then_inc(consts_act, 1)
                    ffn_slot(c, f, role, HEAD if before == "attention" else 0, unused)
                    if isinstance(before, dict) and c < TAIL:
                        ffn_slot(FC + c, **before)
                    if beside:
                        beside(c)
                if role == 2 or splits:
                    nc.scalar.activation(warm[:], minus_half[:, 0:1], ACT.Exp)

            def attention(a, m, beside, before, then):
                for v in range(2 * NT):
                    if before and v < TAIL:
                        ffn_slot(FC + v, **before)
                    t, half = divmod(v, 2)
                    act.wait_ge(v_made, 2 * NT * a + v + 1)
                    nc.scalar.activation(values[:, t, half * N:(half + 1) * N], v_bank[v % 3][:],
                                         ACT.Copy).then_inc(v_copied, 1)

                def exps(s):
                    act.wait_ge(max_ready, PAIRS * a + s + 1)
                    if s >= PR:
                        act.wait_ge(t_made, PAIRS * a + s - PR + 1)
                    for h in range(2):
                        nc.scalar.activation(probs[s % PR][:, h * KEYS:(h + 1) * KEYS], bank[2 + s % 2][:, h * KEYS:(h + 1) * KEYS],
                                             ACT.Exp, bias=neg_max[:, s % 4, h:h + 1],
                                             accum_out=row_sum[:, s % 4, h:h + 1]).then_inc(exp_done, 1)

                def copy_transposed(s):
                    hp, p = divmod(s, NT)
                    act.wait_ge(t_made, PAIRS * a + s + 1)
                    if s >= 2:
                        act.wait_ge(av_done, PAIRS * a + s - 1)
                    nc.scalar.activation(pm_t[hp % 2][:, p * P:(p + 1) * P], bank[4][0:6 * PM, 2 * P:3 * P], ACT.Copy)
                    nc.scalar.activation(probs_t[:, s % 2, :], bank[4][:, 0:2 * P], ACT.Copy).then_inc(t_copied, 1)

                def copy_output(hp):
                    act.wait_ge(av_done, PAIRS * a + NT * (hp + 1))
                    if hp >= 1:
                        act.wait_ge(o_lo, HP * a + hp)
                    nc.scalar.activation(acc[:], bank[5][:], ACT.Copy).then_inc(o_raw, 1)

                def normalise_second(s):
                    act.wait_ge(inv_ready, PAIRS * a + s + 1)
                    part = probs[s % PR][:, KEYS:2 * KEYS]
                    nc.scalar.activation(part, part, ACT.Copy, scale=row_inv[:, s % 4, 1:2]).then_inc(norm_done_act, 1)

                for s in range(SLOTS):
                    if 0 <= s - 1 < ACT_NORMS:
                        normalise_second(s - 1)
                    if s < PAIRS:
                        exps(s)
                    if 0 <= s - T_LAG < PAIRS:
                        copy_transposed(s - T_LAG)
                    if s >= O_LAG and (s - O_LAG) % NT == 0 and (s - O_LAG) // NT < HP:
                        copy_output((s - O_LAG) // NT)
                    if 0 <= s - PAIRS < HEAD:
                        if s == PAIRS:
                            act.wait_ge(k_ready, HP * (a + 1))
                        silu(s - PAIRS, then["f"], then["role"])
                    if s == PAIRS + HEAD:
                        act.wait_ge(wout_done, HP * a + HP - 1)
                        hidden_hi(0, then["f"])
                    beside(s)
                act.wait_ge(wout_done, HP * (a + 1))
                nc.scalar.activation(acc[:], bank[6][:], ACT.Copy).then_inc(yatt_copied, 1)

            def prep(slot, role, n, r, m, src, loads=None):
                for step in steps_of(slot, PREP):
                    if step == "split":
                        act.wait_ge(side_made, m + 1)
                        scale = g_col[:, 0:1] if role == 1 else 1.0
                        nc.scalar.activation(norm_hi[role][:], side[:], ACT.Copy, scale=scale).then_inc(norm_hi_ready, 1)
                    if step == "tanh" and role != 1:
                        act.wait_ge(centred_ready, r + 1)
                        nc.scalar.activation(tanhs[:], centred[:], ACT.Tanh).then_inc(tanh_ready, 1)
                    if step == "gates_split" and role != 1:
                        act.wait_ge(side_made, m + 3)
                        nc.scalar.activation(gates_t[role // 2][0:EXPERTS, :], side[0:EXPERTS, :],
                                             ACT.Copy).then_inc(gates_hi_ready, 1)

            def finish(slot, role, m, count, g):
                pass

            program(nc.scalar, ffn_slot, ffn, attention, prep, finish, start)

        @block.vector
        def _(dve):
            order = split_order()

            def split_block(b, blk):
                slot = b % STAGES
                dve.wait_ge(split_hi, b + 1)
                cols = slice(blk * N, (blk + 1) * N)
                nc.vector.tensor_tensor(w_lo[:, cols], stage(values, slot), w_hi[:, cols].bitcast(F32),
                                        ALU.subtract).then_inc(split_lo, 1)

            def start():
                for i in range(2):
                    nc.vector.memset(gates_t[i][:].bitcast(F32), 0.0)
                    nc.vector.memset(k_diag[i][:], 0.0)

            def split_gate():
                dve.wait_ge(consts_act, 1)
                nc.vector.tensor_tensor(gate_lo[:], gate_raw[:], gate_hi[:].bitcast(F32), ALU.subtract).then_inc(consts_dve, 1)
                dve.wait_ge(consts_pool, 3)
                dve.wait_ge(ld_small, 16 * 3)

            def split_persistent():
                dve.wait_ge(consts_act, 2)
                low = slice(4 * PM, 6 * PM)
                nc.vector.tensor_tensor(pmv_sb[low], pmv_stage(values)[low], pmv_sb[low].bitcast(F32),
                                        ALU.subtract).then_inc(consts_dve, 1)

            def use_output(e, f, role):
                dve.wait_ge(down_done, FC * f + FJ * (e + 1))
                y = y_bank(e, f, role)
                if e == 0:
                    nc.vector.tensor_scalar(acc[:], y, 0.5, None, ALU.mult).then_inc(y_used, 1)
                else:
                    dve.wait_ge(gcols_copied, EXPERTS * f + e)
                    if e >= 3:
                        dve.wait_ge(acc_added, EXPERTS * f + e - 2)
                    nc.vector.tensor_tensor(gated[e % 2], y, gate_cols[e % 2], ALU.mult).then_inc(y_used, 1)

            def ffn_slot(c, f, role, unused=0):
                if c < FC:
                    dve.wait_ge(hid_silu, FC * f + unused + c + 1)
                    halves = FC // 2 * f + FJ // 2 * (c // FJ)
                    if c % FJ in ACT_HI:
                        extra = 1 if unused else 0
                        dve.wait_ge(hid_hi_act, halves + ACT_HI.index(c % FJ) + 1 + extra)
                    else:
                        dve.wait_ge(hid_hi_pool, halves + POOL_HI.index(c % FJ) + 1)
                    wait(dve, down_done, FC * f + c - HR + 1)
                    nc.vector.tensor_tensor(h_lo[:, c % HR, :], hidden[:, c % SR, :],
                                            h_hi[:, c % HR, :].bitcast(F32), ALU.subtract).then_inc(hid_lo, 1)
                if FJ - 1 + LAG <= c < FC + LAG and (c - LAG) % FJ == FJ - 1:
                    use_output((c - LAG) // FJ, f, role)

            def ffn(beside, f, role, m, before, attentions=None, unused=0, splits=False):
                if splits:
                    for b in range(blocks_before(1) + AHEAD):
                        split_block(b, order[b])
                    split_gate()
                for c in range(FC):
                    if splits and split_at(c) is not None:
                        split_block(split_at(c), order[split_at(c)])
                    elif splits and c == LATE:
                        split_persistent()
                    ffn_slot(c, f, role, unused)
                    if isinstance(before, dict) and c < TAIL:
                        ffn_slot(FC + c, **before)
                    if beside:
                        beside(c)

            def attention(a, m, beside, before, then):
                def rotate(w):
                    hp, j = divmod(w, 4)
                    dve.wait_ge(proj_made, UNITS * a + w + 1)
                    if j == 0:
                        wait(dve, q_ready, HP * a + hp)
                    if j == 2:
                        wait(dve, k_ready, HP * a + hp)
                    table = tables[:, j:j + 1, :].broadcast_to([P, 2, N // 2])
                    nc.vector.tensor_tensor(hidden[:, j, :].rearrange("p (b n) -> p b n", b=2),
                                            bank[w % 2][:].rearrange("p (b n) -> p b n", b=2), table,
                                            ALU.mult).then_inc(rot_mul, 1)

                def find_max(s):
                    dve.wait_ge(s_made, PAIRS * a + s + 1)
                    nc.vector.tensor_reduce(neg_max[:, s % 4, :], bank[2 + s % 2][:, 0:2 * KEYS].rearrange(
                        "p (h k) -> p h k", h=2), AX_X, ALU.max, negate=True).then_inc(max_ready, 1)

                def invert_sums(s):
                    dve.wait_ge(exp_done, 2 * (PAIRS * a + s + 1))
                    nc.vector.reciprocal(row_inv[:, s % 4, :], row_sum[:, s % 4, :]).then_inc(inv_ready, 1)

                def normalise(s):
                    dve.wait_ge(inv_ready, PAIRS * a + s + 1)
                    for h in range(1 if s < ACT_NORMS else 2):
                        part = probs[s % PR][:, h * KEYS:(h + 1) * KEYS]
                        last = nc.vector.tensor_scalar(part, part, row_inv[:, s % 4, h:h + 1], None, ALU.mult)
                    last.then_inc(norm_done, 1)

                def persistent_parts(s):
                    return (probs[s % PR][:, PERSISTENT],
                            pm_parts[:, s % 2, :].rearrange("p (i k) -> p i k", i=3))

                def persistent_hi(s):
                    raw, parts = persistent_parts(s)
                    dve.wait_ge(norm_done, PAIRS * a + s + 1)
                    dve.wait_ge(norm_done_act, ACT_NORMS * a + min(s + 1, ACT_NORMS))
                    if s >= 2:
                        dve.wait_ge(t_made, PAIRS * a + s - 1)
                    nc.vector.tensor_copy(parts[:, 0:3:2, :], raw.unsqueeze(1).broadcast_to([P, 2, 2 * PM])).then_inc(parts_hi, 1)

                def persistent_lo(s):
                    raw, parts = persistent_parts(s)
                    dve.wait_ge(parts_hi, PAIRS * a + s + 1)
                    nc.vector.tensor_tensor(parts[:, 1, :], raw, parts[:, 0, :].bitcast(F32), ALU.subtract).then_inc(p_ready, 1)

                def output_low(hp):
                    dve.wait_ge(o_hi, HP * a + hp + 1)
                    nc.vector.tensor_tensor(h_lo[:, OUTPUT_SLOT[hp % 2], :], acc[:], h_hi[:, OUTPUT_SLOT[hp % 2], :].bitcast(F32),
                                            ALU.subtract).then_inc(o_lo, 1)

                def add_first_products(w):
                    wait_apart(dve, (rot_mul, UNITS * a + w + 1))
                    if w == 1:
                        nc.vector.tensor_tensor(q_rot[0], hidden[:, 0, :], hidden[:, 1, :], ALU.add).then_inc(q_ready, 1)
                    else:
                        nc.vector.tensor_tensor(hidden[:, 2, :], hidden[:, 2, :], hidden[:, 3, :],
                                                ALU.add).then_inc(k_added, 1)

                for w in range(LEAD):
                    rotate(w)
                    if before and w < TAIL:
                        ffn_slot(FC + w, **before)
                    if w == 3:
                        add_first_products(3)
                        add_first_products(1)
                for s in range(SLOTS):
                    if s < PAIRS:
                        find_max(s)
                    if ACT_NORMS <= s - 1 < PAIRS:
                        invert_sums(s - 1)
                    if 0 <= s - 1 < PAIRS:
                        normalise(s - 1)
                    if s + LEAD < UNITS:
                        rotate(s + LEAD)
                    if 0 <= s - 1 < PAIRS:
                        persistent_hi(s - 1)
                    if s < ACT_NORMS:
                        invert_sums(s)
                    if 0 <= s - 1 < PAIRS:
                        persistent_lo(s - 1)
                    if s > O_LAG and (s - O_LAG - 1) % NT == 0 and (s - O_LAG - 1) // NT < HP:
                        output_low((s - O_LAG - 1) // NT)
                    beside(s)

            LINKS = 5

            def prep(slot, role, n, r, m, src, loads=None):
                for step in steps_of(slot, PREP):
                    if step == "stats":
                        if role == 0:
                            dve.wait_ge(ld_x, 16 * loads)
                        else:
                            dve.wait_ge(side_used, m)
                        wait(dve, stats_ready, n)
                        for t in range(NT):
                            last = nc.vector.bn_stats(stats[:, t, :], src[:, t, :])
                        last.then_inc(norm_self, 1)
                    if step == "variance":
                        wait_apart(dve, (norm_self, n + 1))
                        for t in range(NT):
                            last = nc.vector.bn_aggr(mean_vars[role % 2][:, t, :], stats[:, t, :])
                        last.then_inc(stats_ready, 1)
                    if step in ("x_hat", "x_hat_rest"):
                        if step == "x_hat":
                            dve.wait_ge(rstd_ready, n + 1)
                        for t in range(NT // 2) if step == "x_hat" else range(NT // 2, NT):
                            last = nc.vector.tensor_scalar(x_hat[:, t, :], src[:, t, :], mean_vars[role % 2][:, t, 0:1],
                                                           rstd[:, 1, t:t + 1], ALU.subtract, ALU.mult)
                        if step == "x_hat_rest":
                            last.then_inc(xhat_ready, 1)
                    if step == "split":
                        dve.wait_ge(norm_hi_ready, n + 1)
                        high = norm_hi[role][:].bitcast(F32)
                        if role == 1:
                            nc.vector.scalar_tensor_tensor(norm_lo[role][:], side[:], g_col[:, 0:1], high,
                                                           ALU.mult, ALU.subtract).then_inc(side_used, 1)
                        else:
                            nc.vector.tensor_tensor(norm_lo[role][:], side[:], high, ALU.subtract).then_inc(side_used, 1)
                    if role == 1:
                        continue
                    def link(ins, done):
                        ins.then_inc(prep_self, 1)
                        dve.wait_ge(prep_self, LINKS * r + done)
                    if step == "copy":
                        dve.wait_ge(side_made, m + 2)
                        nc.vector.tensor_copy(logits[:], side[:, 0:NT * EXPERTS].rearrange(
                            "p (t e) -> p t e", t=NT)).then_inc(side_used, 1)
                    if step == "compare":
                        wait_apart(dve, (side_used, m + 2))
                        other = logits[:].unsqueeze(2).broadcast_to([P, NT, EXPERTS, EXPERTS])
                        own = logits[:].unsqueeze(3).broadcast_to([P, NT, EXPERTS, EXPERTS])
                        for t in range(NT):
                            last = nc.vector.max(top8[:, t, :], logits[:, t, :])
                        nc.vector.tensor_tensor(cmp_ge, other, own, ALU.is_ge)
                        link(nc.vector.tensor_tensor(cmp_gt, other, own, ALU.is_gt), 1)
                    if step == "ties":
                        tie = below[:].unsqueeze(1).broadcast_to([P, NT, EXPERTS, EXPERTS])
                        rest = above[:].unsqueeze(1).broadcast_to([P, NT, EXPERTS, EXPERTS])
                        nc.vector.tensor_tensor(cmp_ge, cmp_ge, tie, ALU.mult)
                        link(nc.vector.tensor_tensor(cmp_gt, cmp_gt, rest, ALU.mult), 2)
                    if step == "rank":
                        link(nc.vector.tensor_tensor(cmp_gt, cmp_gt, cmp_ge, ALU.add), 3)
                        link(nc.vector.tensor_reduce(rank[:], cmp_gt, AX_X, ALU.add), 4)
                    if step == "chosen":
                        nc.vector.tensor_scalar(rank[:], rank[:], 2.0, 0.25, ALU.is_lt, ALU.mult)
                        link(nc.vector.tensor_tensor(top_sum[:], top8[:, :, 0:1], top8[:, :, 1:2], ALU.add), 5)
                    if step == "centre":
                        nc.vector.scalar_tensor_tensor(centred[:], top_sum[:].broadcast_to([P, NT, EXPERTS]), -0.5,
                                                       logits[:], ALU.mult, ALU.add).then_inc(centred_ready, 1)
                    if step == "gates":
                        dve.wait_ge(tanh_ready, r + 1)
                        nc.vector.scalar_tensor_tensor(gates[:], tanhs[:], 1.0, rank[:], ALU.add,
                                                       ALU.mult).then_inc(gates_ready, 1)
                    if step == "gates_split":
                        dve.wait_ge(gates_hi_ready, r + 1)
                        part = gates_t[role // 2]
                        nc.vector.tensor_tensor(part[32:32 + EXPERTS, :], side[0:EXPERTS, :],
                                                part[0:EXPERTS, :].bitcast(F32), ALU.subtract).then_inc(side_used, 1)

            def finish(slot, role, m, count, g):
                for step in steps_of(slot, FINISH):
                    if step == "add":
                        dve.wait_ge(side_made, m + 1)
                        old, new = ((x1, x2), (x2, x3), (x3, x3))[role]
                        if role == 1:
                            dve.wait_ge(st_out, 16 * g + 16)
                        nc.vector.tensor_tensor(new[:], side[:].rearrange("p (t d) -> p t d", t=NT), old[:],
                                                ALU.add).then_inc(side_used, 1)

            program(nc.vector, ffn_slot, ffn, attention, prep, finish, start)

        @block.gpsimd
        def _(pool):
            done = [0]

            def link(ins):
                done[0] += 1
                ins.then_inc(pool_self, 1)
                pool.wait_ge(pool_self, done[0])

            def start():
                nc.gpsimd.memset(minus_half[:], -0.5)
                link(nc.gpsimd.memset(ident[:], 0.0))
                nc.gpsimd.affine_select(out=ident[:], in_=ident[:], compare_op=ALU.not_equal, fill=1.0, base=0,
                                        pattern=[[-1, P]], channel_multiplier=1).then_inc(consts_pool, 1)
                link(nc.gpsimd.memset(pick_raw[:], 0.0))
                link(nc.gpsimd.affine_select(out=pick_raw[:], in_=pick_raw[:], compare_op=ALU.not_equal, fill=1.0,
                                             base=0, pattern=[[-1, EXPERTS]], channel_multiplier=1))
                nc.gpsimd.affine_select(out=pick_raw[:], in_=pick_raw[:], compare_op=ALU.not_equal, fill=1.0,
                                        base=-32, pattern=[[-1, EXPERTS]], channel_multiplier=1).then_inc(consts_pool, 1)
                pool.wait_ge(consts_pool, 2)

            def later_constants():
                nc.gpsimd.memset(below[:], 1.0)
                link(nc.gpsimd.memset(above[:], 1.0))
                for x, sign in ((below, 1), (above, -1)):
                    nc.gpsimd.affine_select(out=x[:], in_=x[:], compare_op=ALU.is_gt, fill=0.0, base=0,
                                            pattern=[[sign, EXPERTS], [-sign, EXPERTS]], channel_multiplier=0)
                nc.gpsimd.memset(ident_bf[:], 0.0)
                link(nc.gpsimd.memset(mask_bf[:], 0.0))
                link(nc.gpsimd.affine_select(out=ident_bf[:], in_=ident_bf[:], compare_op=ALU.not_equal, fill=1.0,
                                             base=0, pattern=[[-1, P]], channel_multiplier=1))
                for at in OWN:
                    own = mask_bf[:, at:at + P]
                    link(nc.gpsimd.affine_select(out=own, in_=own, compare_op=ALU.is_ge, fill=MASKED, base=0,
                                                 pattern=[[-1, P]], channel_multiplier=1))
                    link(nc.gpsimd.memset(mask_bf[SEG:P, at:at + SEG], MASKED))
                for quarter, (first, second) in enumerate(((1.0, 0.0), (0.0, 1.0), (1.0, 0.0), (0.0, 1.0))):
                    rows = slice(quarter * 32, (quarter + 1) * 32)
                    link(nc.gpsimd.memset(head_rows[rows, 0:1], first))
                    link(nc.gpsimd.memset(head_rows[rows, 1:2], second))
                pool.sem_inc(consts_pool, 1)
                pool.wait_ge(ld_small, 16 * 3)

            def add_output(e, f):
                pool.wait_ge(y_used, FE * f + e + 1)
                if e >= 2:
                    pool.wait_ge(acc_added, EXPERTS * f + e - 1)
                nc.gpsimd.tensor_tensor(acc[:], acc[:], gated[e % 2], ALU.add).then_inc(acc_added, 1)

            def ffn_slot(c, f, role, unused=0):
                if c < FC and c % FJ in POOL_HI:
                    wait_apart(pool, (hid_silu, FC * f + unused + c + 1), (down_done, FC * f + c - HR + 1))
                    nc.gpsimd.tensor_scalar(h_hi[:, c % HR, :], hidden[:, c % SR, :], 1.0, 1.0,
                                            ALU.mult, ALU.mult).then_inc(hid_hi_pool, 1)
                d = c - LAG - 1
                if d >= 2 * FJ - 1 and d % FJ == FJ - 1:
                    add_output(d // FJ, f)

            def ffn(beside, f, role, m, before, attentions=None, unused=0, splits=False):
                if splits:
                    later_constants()
                if before == "attention":
                    pool.wait_ge(av_done, PAIRS * attentions)
                for c in range(FC):
                    if before == "attention" and c == OUTPUT_SLOT[1]:
                        pool.wait_ge(wout_done, HP * attentions)
                    ffn_slot(c, f, role, unused)
                    if isinstance(before, dict) and c < TAIL:
                        ffn_slot(FC + c, **before)
                    if beside:
                        beside(c)

            def attention(a, m, beside, before, then):
                def add_products(w):
                    hp, j = divmod(w, 4)
                    if j == 1 and hp > 0:
                        pool.wait_ge(rot_mul, UNITS * a + w + 1)
                        if hp >= 2:
                            pool.wait_ge(s_made, PAIRS * a + NT * (hp - 1))
                        nc.gpsimd.tensor_tensor(q_rot[hp % 2], hidden[:, 0, :], hidden[:, 1, :],
                                                ALU.add).then_inc(q_ready, 1)
                    if j == 3:
                        if hp > 0:
                            pool.wait_ge(rot_mul, UNITS * a + w + 1)
                            nc.gpsimd.tensor_tensor(hidden[:, 2, :], hidden[:, 2, :], hidden[:, 3, :],
                                                    ALU.add).then_inc(k_added, 1)
                        if hp >= 2:
                            pool.wait_ge(s_made, PAIRS * a + NT * (hp - 1))
                        wait_apart(pool, (k_added, HP * a + hp + 1))
                        for h in range(2):
                            nc.gpsimd.tensor_scalar(k_diag[hp % 2][:, :, OWN[h]:OWN[h] + P],
                                                    hidden[:, 2, :].rearrange("p (t n) -> p t n", t=NT),
                                                    head_rows[:, h:h + 1], 1.0, ALU.mult, ALU.mult)
                        nc.gpsimd.tensor_scalar(k_diag[hp % 2][:, :, PERSISTENT],
                                                pmk_sb[:, hp:hp + 1, :].broadcast_to([P, NT, 2 * PM]),
                                                1.0, 1.0, ALU.mult, ALU.mult).then_inc(k_ready, 1)

                def output_hi(hp):
                    waits = [(o_raw, HP * a + hp + 1)]
                    if hp >= 2:
                        waits.append((wout_done, HP * a + hp - 1))
                    wait_apart(pool, *waits)
                    nc.gpsimd.tensor_scalar(h_hi[:, OUTPUT_SLOT[hp % 2], :], acc[:], 1.0, 1.0, ALU.mult, ALU.mult).then_inc(o_hi, 1)

                if before:
                    for c in range(FC, FC + TAIL):
                        ffn_slot(c, **before)
                for w in range(LEAD):
                    add_products(w)
                for s in range(SLOTS):
                    if s >= O_LAG and (s - O_LAG) % NT == 0 and (s - O_LAG) // NT < HP:
                        output_hi((s - O_LAG) // NT)
                    if s + LEAD < UNITS:
                        add_products(s + LEAD)
                    beside(s)

            def prep(slot, role, n, r, m, src, loads=None):
                for step in steps_of(slot, PREP):
                    if step == "rstd":
                        wait_apart(pool, (stats_ready, n + 1), (xhat_ready, n))
                        factor, term = (1 + RMS_EPS, LN_EPS * RMS_EPS) if role == 1 else (1.0, LN_EPS)
                        nc.gpsimd.tensor_scalar(rstd[:, 0, :], mean_vars[role % 2][:, :, 1], factor, term,
                                                ALU.mult, ALU.add).then_inc(rstd_self, 1)
                        wait_apart(pool, (rstd_self, n + 1))
                        nc.gpsimd.tensor_tensor(rstd[:, 1, :], rstd[:, 0, :], minus_half[:], ALU.pow).then_inc(rstd_ready, 1)

            def finish(slot, role, m, count, g):
                pass

            program(nc.gpsimd, ffn_slot, ffn, attention, prep, finish, start)


def stage(values, slot):
    return values[:, slot // 2, slot % 2 * N:(slot % 2 + 1) * N]


def pmv_stage(values):
    return values[0:96, NT - 1, :].rearrange("p (h d) -> p h d", h=HP)


def blocks_before(experts):
    rest = BLOCKS - Q_AT
    experts = min(experts, FE)
    return 2 * experts + (rest * (experts - 1) + FE - 2) // (FE - 1)


def split_at(c):
    e, j = divmod(c + AHEAD, FJ)
    b = blocks_before(e + 1) + j
    return b if b < blocks_before(e + 2) else None


def split_order():
    order = []
    for e in range(FE):
        order += [2 * e, 2 * e + 1]
        while len(order) < blocks_before(e + 1):
            order.append(Q_AT + len(order) - 2 * (e + 1))
    return order


def kernel(L0_attn_seq, L0_attn_g_norm, L0_attn_W_qkv, L0_attn_W_out, L0_attn_pm,
           L0_ffn_shared_w1, L0_ffn_shared_w2, L0_ffn_experts_w1, L0_ffn_experts_w2, L0_ffn_gate_w):
    import numpy as np
    import concourse.bacc as bacc
    from concourse import mybir as mb
    from concourse.bass_utils import run_bass_kernel_spmd

    seq, wqkv, wout, pm = (np.asarray(a) for a in (L0_attn_seq, L0_attn_W_qkv, L0_attn_W_out, L0_attn_pm))
    b, s, d = seq.shape
    groups = b * s // N
    x = seq.reshape(groups, NT, P, d).transpose(0, 2, 1, 3)
    shape = x.shape
    x = np.concatenate([x, x[:1]])

    half = np.arange(DH // 2)
    channel = np.concatenate([2 * half, 2 * half, 2 * half + 1, 2 * half + 1])
    head = np.repeat([0, 1, 0, 1], DH // 2)
    cols = (np.arange(HP)[:, None] * 2 + head) * DH + channel
    cols = np.concatenate([cols, cols[:, :DH]], axis=1).reshape(-1)
    inner = HEADS * DH
    w1 = np.concatenate([np.asarray(L0_ffn_shared_w1)[None], np.asarray(L0_ffn_experts_w1)])
    w2 = np.concatenate([np.asarray(L0_ffn_shared_w2)[None], np.asarray(L0_ffn_experts_w2)])
    w1 = w1.transpose(2, 0, 1)
    w2 = w2.reshape(FE, d, FJ, P).transpose(3, 0, 2, 1).reshape(P, FE, FJ * d)
    experts = np.stack([w1, w2], axis=2).reshape(P, -1)
    weights = np.concatenate([experts, wqkv[:, cols], wqkv[:, inner + cols], wqkv[:, 2 * inner:],
                              wout.reshape(HP, P, d).transpose(1, 0, 2).reshape(P, -1)], axis=1)

    pm_k = np.zeros((P, HP, 2, PM), pm.dtype)
    pm_v = np.zeros((3, 2, PM, HP, 2, DH), pm.dtype)
    for h in range(2):
        pm_k[head == h, :, h, :] = pm[0, h::2][:, :, channel[head == h]].transpose(2, 0, 1)
        pm_v[:, h, :, :, h, :] = pm[1, h::2].transpose(1, 0, 2)
    pm_k, pm_v = pm_k.reshape(P, HP, 2 * PM), pm_v.reshape(96, HP, P)

    freq = np.float32(1) / np.float32(10000.0) ** (np.arange(0, DH, 2, dtype=np.float32) / np.float32(DH))
    angle = (np.arange(s, dtype=np.float32)[:, None] * freq).T.astype(np.float32)
    angle = angle[channel // 2]
    cos, sin = np.cos(angle), np.where(channel[:, None] % 2, np.sin(angle), -np.sin(angle))
    rotary = np.stack([cos * DH ** -0.5, sin * DH ** -0.5, cos, sin], axis=1).astype(np.float32)

    ins = {"x": x, "weights": weights, "gate_w": np.asarray(L0_ffn_gate_w).T, "g_norm": np.asarray(L0_attn_g_norm)[:, None],
           "pm_k": pm_k, "pm_v": pm_v, "rotary": rotary}
    nc = bacc.Bacc("TRN2", target_bir_lowering=False, num_devices=1)
    arrays, args = {}, []
    for name, a in ins.items():
        arrays[name] = np.ascontiguousarray(a)
        args.append(nc.dram_tensor(name, a.shape, mb.dt.from_np(a.dtype), kind="ExternalInput").ap())
    args.append(nc.dram_tensor("out", shape, mb.dt.float32, kind="ExternalOutput").ap())
    macaron(nc, *args)
    r = run_bass_kernel_spmd(nc, [arrays], core_ids=[0])
    out = np.asarray(r.results[0]["out"])
    return out.transpose(0, 2, 1, 3).reshape(b, s, d)
```
